# Optimizing a Trainium2 kernel written in Bass

```python
import numpy as np
import jax
import jax.numpy as jnp

def _softmax(x, axis=-1):
    return jax.nn.softmax(x, axis=axis)

def _gelu(x):
    return jax.nn.gelu(x, approximate=True)

def _silu(x):
    return jax.nn.silu(x)

def _sigmoid(x):
    return jax.nn.sigmoid(x)

def _layernorm(x, axis=-1, eps=1e-05):
    m = jnp.mean(x, axis=axis, keepdims=True)
    v = jnp.var(x, axis=axis, keepdims=True)
    return (x - m) / jnp.sqrt(v + eps)

def _scatter_add(tgt, idx, src, axis=0):
    return tgt.at[idx].add(src)

def _segment_sum(src, seg, n):
    return jax.ops.segment_sum(src, seg, n)
kernel_name = 'mk_flamingo_gated_d1_seqx_r4_712323'

def setup_inputs(seed: int=0):
    np.random.seed(seed)
    _w = jnp.asarray

    def _rec_inputs():
        import jax
        import jax.numpy as jnp
        _rk = jax.random.key(seed)
        x = -0.000125 + 0.9999 * jax.random.normal(jax.random.fold_in(_rk, 1), (2, 1024, 256), jnp.float32)
        _lenS = 1024 - jax.random.randint(jax.random.fold_in(_rk, 7), (2,), 0, max(1, 1024 // 4) + 1, jnp.int32)
        _lenS2 = 77 - jax.random.randint(jax.random.fold_in(_rk, 8), (2,), 0, max(1, 77 // 4) + 1, jnp.int32)
        _ctx_1024P = jax.random.normal(jax.random.fold_in(_rk, 11), (2, 16, 256), jnp.float32)
        _ctx_1024c = jax.random.dirichlet(jax.random.fold_in(_rk, 511), 0.3 * jnp.ones((16,), jnp.float32), (2, 77))
        _ctx_1024t = jnp.einsum('bsk,bkd->bsd', _ctx_1024c, _ctx_1024P)
        _ctx_1024t = _ctx_1024t * jax.lax.rsqrt(jnp.mean(jnp.square(_ctx_1024t)) + 1e-12) * 0.953939
        ctx_1024 = -1.52775e-05 + 0.999936 * (_ctx_1024t + 0.3 * jax.random.normal(jax.random.fold_in(_rk, 611), (2, 77, 256), jnp.float32))
        _validS = jnp.arange(1024)[None, :] < _lenS[:, None]
        _validS2 = jnp.arange(77)[None, :] < _lenS2[:, None]
        _causal = jnp.tril(jnp.ones((1024, 1024), dtype=bool))
        mask_BxS2_bk0 = jnp.logical_not(jnp.broadcast_to(_validS2[:, :], (2, 77)))
        _g = jax.random.normal(jax.random.fold_in(_rk, 9001), (2, 1), jnp.float32)
        _g = jnp.sign(_g) * jnp.maximum(jnp.abs(_g), 1.0) + (_g == 0) * 1.0
        g_xattn = _g[0]
        g_ffn = _g[1]
        return (x, ctx_1024, mask_BxS2_bk0, g_xattn, g_ffn)
    x, ctx_1024, mask_BxS2_bk0, g_xattn, g_ffn = _rec_inputs()

    def _L0_xattn_setup():
        import jax, jax.numpy as jnp
        import numpy as np
        B, L1, L2, H = (16, 512, 512, 256)
        key = jax.random.key(seed)
        kx, ky, km, kw, kb = jax.random.split(key, 5)
        x = jax.random.normal(kx, (B, L1, H), dtype=jnp.float32)
        y = jax.random.normal(ky, (B, L2, H), dtype=jnp.float32)
        y_mask = jax.random.randint(km, (B, L2), 0, 8) == 0
        stdv = 1.0 / np.sqrt(H)
        W = jax.random.uniform(kw, (H, H), minval=-stdv, maxval=stdv, dtype=jnp.float32)
        b = jax.random.uniform(kb, (H,), minval=-stdv, maxval=stdv, dtype=jnp.float32)
        return {'x': x, 'y': y, 'y_mask': y_mask, 'W': W, 'b': b}
    _L0_xattn_all = _L0_xattn_setup()
    _L0_xattn_in = {k: v for k, v in _L0_xattn_all.items() if k in ('W', 'b')}
    del _L0_xattn_all

    def _L0_ffn_setup():
        import jax, jax.numpy as jnp
        import numpy as np
        E = 8
        TOPK = 2
        H = 256
        I = 256
        ISH = I * 2
        B, S = (2, 256)
        key = jax.random.key(seed)
        ks = jax.random.split(key, 7)
        s = 0.02
        return {'hidden_states': jax.random.normal(ks[0], (B, S, H), jnp.float32), 'w_router': jax.random.normal(ks[1], (H, E), jnp.float32) * s, 'fc1_w': jax.random.normal(ks[2], (E, H, 2 * I), jnp.float32) * s, 'fc2_w': jax.random.normal(ks[3], (E, I, H), jnp.float32) * s, 'gate_w': jax.random.normal(ks[4], (H, ISH), jnp.float32) * s, 'up_w': jax.random.normal(ks[5], (H, ISH), jnp.float32) * s, 'down_w': jax.random.normal(ks[6], (ISH, H), jnp.float32) * s}
    _L0_ffn_all = _L0_ffn_setup()
    _L0_ffn_in = {k: v for k, v in _L0_ffn_all.items() if k in ('w_router', 'fc1_w', 'fc2_w', 'gate_w', 'up_w', 'down_w')}
    del _L0_ffn_all
    return {'x': x, 'ctx_1024': ctx_1024, 'mask_BxS2_bk0': mask_BxS2_bk0, 'g_xattn': g_xattn, 'g_ffn': g_ffn, 'L0_xattn_W': _L0_xattn_in['W'], 'L0_xattn_b': _L0_xattn_in['b'], 'L0_ffn_w_router': _L0_ffn_in['w_router'], 'L0_ffn_fc1_w': _L0_ffn_in['fc1_w'], 'L0_ffn_fc2_w': _L0_ffn_in['fc2_w'], 'L0_ffn_gate_w': _L0_ffn_in['gate_w'], 'L0_ffn_up_w': _L0_ffn_in['up_w'], 'L0_ffn_down_w': _L0_ffn_in['down_w']}

def reference(x, ctx_1024, mask_BxS2_bk0, g_xattn, g_ffn, L0_xattn_W, L0_xattn_b, L0_ffn_w_router, L0_ffn_fc1_w, L0_ffn_fc2_w, L0_ffn_gate_w, L0_ffn_up_w, L0_ffn_down_w):
    import jax
    import jax.numpy as jnp

    def _L0_xattn_ref(x, y, y_mask, W, b):
        import jax, jax.numpy as jnp
        import numpy as np
        B, L1, L2, H = (16, 512, 512, 256)
        x_proj = jax.nn.relu(jnp.einsum('bih,oh->bio', x, W) + b)
        y_proj = jax.nn.relu(jnp.einsum('bjh,oh->bjo', y, W) + b)
        scores = jnp.einsum('bih,bjh->bij', x_proj, y_proj)
        scores = jnp.where(y_mask[:, None, :], -jnp.inf, scores)
        alpha = jax.nn.softmax(scores, axis=-1)
        matched_seq = jnp.einsum('bij,bjh->bih', alpha, y)
        return matched_seq

    def _L0_ffn_ref(hidden_states, w_router, fc1_w, fc2_w, gate_w, up_w, down_w):
        import jax, jax.numpy as jnp
        import numpy as np
        E = 8
        TOPK = 2
        H = 256
        I = 256
        ISH = I * 2
        B, S = (2, 256)
        orig_shape = hidden_states.shape
        x = hidden_states.reshape(-1, orig_shape[-1])
        logits = x @ w_router
        top_logits, top_idx = jax.lax.top_k(logits, TOPK)
        scores = jax.nn.softmax(top_logits, axis=-1)
        flat_idx = top_idx.reshape(-1)
        sorted_idx = jnp.argsort(flat_idx)
        permuted = x[sorted_idx // TOPK]
        eid = flat_idx[sorted_idx]
        out_perm = jnp.zeros((permuted.shape[0], orig_shape[-1]), x.dtype)
        for e in range(E):
            m = (eid == e).astype(x.dtype)[:, None]
            h1 = permuted * m @ fc1_w[e]
            proj, gate = jnp.split(h1, 2, axis=-1)
            out_perm = out_perm + jax.nn.silu(proj) * gate @ fc2_w[e]
        unperm = jnp.zeros_like(out_perm).at[sorted_idx].set(out_perm)
        moe_out = (unperm.reshape(-1, TOPK, orig_shape[-1]) * scores[:, :, None]).sum(axis=1)
        moe_out = moe_out.reshape(orig_shape)
        shared = jax.nn.silu(hidden_states @ gate_w) * (hidden_states @ up_w) @ down_w
        return moe_out + shared
    x = x + jnp.tanh(g_xattn[0]) * _L0_xattn_ref(_layernorm(x, axis=-1), ctx_1024, mask_BxS2_bk0, L0_xattn_W, L0_xattn_b)
    x = x + jnp.tanh(g_ffn[0]) * _L0_ffn_ref(_layernorm(x, axis=-1), L0_ffn_w_router, L0_ffn_fc1_w, L0_ffn_fc2_w, L0_ffn_gate_w, L0_ffn_up_w, L0_ffn_down_w)
    return x

_drawn_inputs = setup_inputs


def setup_inputs(seed=0):
    import zlib

    import numpy as np

    out = dict(_drawn_inputs(seed))
    spreads = {}
    factors = {'L0_ffn_w_router': 7.616,
     'L0_ffn_fc1_w': 6.574,
     'L0_ffn_fc2_w': 6.602,
     'L0_ffn_gate_w': 3.303,
     'L0_ffn_up_w': 3.307,
     'L0_ffn_down_w': 3.268}
    for name, (base, spread) in spreads.items():
        noise = np.random.default_rng([zlib.crc32(name.encode()), seed]).standard_normal(out[name].shape)
        drawn = base * np.exp(spread * noise) if base else spread * noise
        out[name] = jnp.asarray(drawn.astype(out[name].dtype))
    for name, factor in factors.items():
        out[name] = (out[name] * factor).astype(out[name].dtype)
    return out
```

```python
import concourse.bass as bass
from concourse import mybir
from contextlib import ExitStack

F32 = mybir.dt.float32
F32R = mybir.dt.float32r
BF16 = mybir.dt.bfloat16
I32 = mybir.dt.int32
U8 = mybir.dt.uint8
ALU = mybir.AluOpType
ACT = mybir.ActivationFunctionType
X = mybir.AxisListType.X

P = 128
B, S, D = 2, 1024, 256
J, JP = 77, 80
E, I = 8, 256
F = 512
TOK = B * S
GT = 4
GN = GT * P
NG = TOK // GN
NT = TOK // P
K = D // P
FC = F // P
REGION = TOK + P
PAD_ROW = E * REGION
ROW = D + 2
N_TILES = (2 * TOK + E * (P - 1)) // P
NOWHERE = 1.0e6
BIG = 1.0e30
EPS = 1e-5
WCH = 3 * E
N_CONST = 6
RT = 17
SL = 5
CPI = WCH // (NG - 1)


def build(nc, x, ctx_in, mask, g_xattn, g_ffn, W, bvec, w_router, fc1, fc2, gate_w, up_w, down_w, out):
    rows = nc.dram_tensor("rows", [PAD_ROW + P, ROW], F32).ap()
    parts = nc.dram_tensor("parts", [2 * TOK, D], F32).ap()
    x_v = x.rearrange("b (t p) d -> p (b t) d", p=P)
    out_v = out.rearrange("b (t p) d -> p (b t) d", p=P)
    parts_v = parts.rearrange("(k t p) d -> k p t d", k=2, p=P)

    with ExitStack() as ctx:
        def sb(name, shape, dt=F32):
            return ctx.enter_context(nc.sbuf_tensor(name, shape, dt))

        def sem(name):
            return ctx.enter_context(nc.semaphore(name))

        ew_hi = sb("ew_hi", [P, WCH, 512], F32R)
        ew_lo = sb("ew_lo", [P, WCH, 512], F32R)
        sw_hi = sb("sw_hi", [P, 6, 512], F32R)
        sw_lo = sb("sw_lo", [P, 6, 512], F32R)
        wt_hi = sb("wt_hi", [P, K, D], F32R)
        wt_lo = sb("wt_lo", [P, K, D], F32R)
        y_hi = sb("y_hi", [JP, B, D], F32R)
        y_lo = sb("y_lo", [JP, B, D], F32R)
        yp_hi = sb("yp_hi", [P, K, B, JP], F32R)
        yp_lo = sb("yp_lo", [P, K, B, JP], F32R)
        wr_hi = sb("wr_hi", [P, K, E], F32R)
        wr_lo = sb("wr_lo", [P, K, E], F32R)
        acc = sb("acc", [P, NT, D])
        xn = sb("xn", [P, GT, D])
        hr = sb("hr", [P, GT, ROW])
        ht_hi = sb("ht_hi", [P, K, GN], F32R)
        ht_lo = sb("ht_lo", [P, K, GN], F32R)
        xt_hi = sb("xt_hi", [P, K, GN], F32R)
        xt_lo = sb("xt_lo", [P, K, GN], F32R)
        xp_hi = sb("xp_hi", [P, K, GN], F32R)
        xp_lo = sb("xp_lo", [P, K, GN], F32R)
        xp = sb("xp", [P, K, GN])
        act = sb("act", [P, 2, GN])
        act_hi = sb("act_hi", [P, 2, GN], F32R)
        act_lo = sb("act_lo", [P, 2, GN], F32R)
        stage = sb("stage", [P, 2, 512])
        s_in = sb("s_in", [P, GT, JP])
        s_exp = s_in
        ident = sb("ident", [P, P])
        ones = sb("ones", [P, P], BF16)
        before = sb("before", [P, P], BF16)
        row = act[0:1, 0, 0:2 * JP + 2]
        ones_row = act[0:1, 1, 0:P]
        mrow = sb("mrow", [1, B * J], U8)
        mbias = sb("mbias", [P, B, JP])
        tg = sb("tg", [P, 2])
        bcol = sb("bcol", [P, K])
        wr_raw = sb("wr_raw", [P, K, E])
        half = sb("half", [P, GT])
        st1 = sb("st1", [P, NT, 6])
        mv1 = sb("mv1", [P, NT, 2])
        rs1 = sb("rs1", [P, NT])
        st2 = sb("st2", [P, GT, 6])
        mv2 = sb("mv2", [P, GT, 2])
        rs2 = sb("rs2", [P, GT])
        ve1 = sb("ve1", [P, NT])
        ve2 = sb("ve2", [P, GT])
        s_max = sb("s_max", [P, GT])
        s_sum = sb("s_sum", [P, GT])
        s_inv = sb("s_inv", [P, GT])
        s_coef = sb("s_coef", [P, GT])
        lg = sb("lg", [P, GT, E])
        lg2 = sb("lg2", [P, GT, E])
        q1 = sb("q1", [P, GT, E])
        q2 = sb("q2", [P, GT, E])
        oh1 = sb("oh1", [P, GT, E])
        oh2 = sb("oh2", [P, GT, E])
        pick = sb("pick", [P, GT, E], BF16)
        i1 = sb("i1", [P, GT])
        i2 = sb("i2", [P, GT])
        mx = sb("mx", [P, 2, NT])
        seen = sb("seen", [P, NT + 1, E], BF16)
        place = sb("place", [P, GT, E])
        slotf = sb("slotf", [P, 2, GT])
        slot = sb("slot", [P, 2, GT], I32)
        e_m8 = sb("e_m8", [P, E])
        e_reg = sb("e_reg", [P, E])
        tokf = sb("tokf", [P, NT])
        wsm = sb("wsm", [P, 6, NT])
        cnt = sb("cnt", [P, E])
        cnti = sb("cnti", [P, 3, E], I32)
        cum = sb("cum", [P, 5, E + 1])
        tix = sb("tix", [P, N_TILES])
        e9 = sb("e9", [P, E + 1])
        n9 = N_TILES * (E + 1)
        xn_flat = xn[:].rearrange("p t d -> p (t d)")
        cmp9 = xn_flat[:, 0:n9].rearrange("p (t e) -> p t e", e=E + 1)
        cmp9b = xn_flat[:, n9:2 * n9].rearrange("p (t e) -> p t e", e=E + 1)
        pad_rows = xn_flat[:, 2 * n9:2 * n9 + ROW]
        t_exp = sb("t_exp", [P, N_TILES])
        t_w = sb("t_w", [P, N_TILES], I32)
        t_off = sb("t_off", [P, N_TILES], I32)
        t_offf = sb("t_offf", [P, N_TILES])
        dst_tmp = sb("dst_tmp", [P, N_TILES])
        dstf = sb("dstf", [P, N_TILES])
        dst = [sb(f"dst{i}", [P, 1], I32) for i in range(2)]

        bank = [ctx.enter_context(nc.psum_tensor(f"bank{i}", [P, 512], F32)) for i in range(8)]
        BG, BU, BD = bank[4], bank[5], bank[6:8]

        names = """const_z const_p const_v x_raw rstd1 rstd2 row_built
            wt_ps wt_h wt_l y_h y_l yT_ps yT_h yT_l yp_ps yp_r yp_h yp_l wr_h wr_l row_ps row_bc
            stats1 mean1 xn_ready xt_ps xt_h xt_l xp_ps xp_r xp_h xp_l
            sc_ps sc_in sc_max sc_sub sc_exp sc_sum sc_inv sc_coef eT_ps eT_h eT_l mt_ps resid
            stats2 mean2 h_ready hT_ps hT_h hT_l lg_ps rt rank_ps slots row_fields scattered
            gu_ps sil prod act_h act_l dn_ps dn_added cnt_ps pads tb tiles_known weights_w
            xT_ps xT_h xT_l h1_ps m_sil m_prod aT_ps aT_h aT_l y2_ps y_sb dst_t dst_f dst_i
            done outs sl_step w_tanh comb pad_rows passed pow1 pow2 chunk_h chunk_l""".split()
        s = {n: sem(n) for n in names}
        x_in = [sem(f"x_in{g}") for g in range(NG)]
        w_in, y_in, small_in, mask_in, sm2_in = (sem(n) for n in ("w_in", "y_in", "small_in", "mask_in", "sm2_in"))
        stage_in = [sem(f"stage_in{i}") for i in range(2)]
        tile_in = [sem(f"tile_in{i}") for i in range(2)]
        part_out = [sem(f"part_out{i}") for i in range(2)]
        part_in = [sem(f"part_in{g}") for g in range(NG)]

        ahead = {"act_l": 2, "dn_ps": 2, "prod": 1, "dn_added": 1}

        def give(eng, *which):
            for name in which:
                eng.sem_inc(s[name], ahead[name])

        def after(eng, name, value):
            if not (isinstance(value, int) and value <= 0):
                eng.wait_ge(s[name], value + ahead.get(name, 0))

        def apart(eng, name, value):
            after(eng, name, value)
            eng.sem_inc(s["passed"], 1)

        def bc_mid(ap, n):
            return ap.unsqueeze(1).broadcast_to([ap.shape[0], n, ap.shape[1]])

        def bc_last(ap, n):
            return ap.unsqueeze(2).broadcast_to([ap.shape[0], ap.shape[1], n])

        def at(t3, i):
            return t3[:, bass.ds(i, 1), :].rearrange("p a d -> p (a d)")

        def mm3(pe, ps, lhs, rhs, chunks, first=True, last=True, lone=True):
            n, total, ins = 0, 3 * chunks, None
            for k in range(chunks):
                (lh, ll), (rh, rl) = lhs(k), rhs(k)
                for a, b in ((lh, rh), (lh, rl), (ll, rh)):
                    ins = pe.matmul(ps, a, b, start=first and n == 0, stop=last and n == total - 1,
                                    skip_group_check=not lone)
                    n += 1
            return ins

        def part_buf(g):
            tiles = lambda b: b[:].rearrange("p a n -> p (a n)").rearrange("p (t d) -> p t d", d=D)
            return (xn[:, :, :], tiles(xp)) if g % 2 == 0 else (hr[:, :, 0:D], tiles(act))

        block = ctx.enter_context(nc.Block())

        @block.sync
        def _(sp):
            sp.dma_start(acc[:, 0:GT, :], x_v[:, 0:GT, :]).then_inc(x_in[0], 16)
            sp.dma_start(stage[:, :, :].rearrange("p k (o h) -> p (k o) h", h=D)[:, 0:K, :],
                         W.rearrange("(t p) h -> p t h", p=P)).then_inc(w_in, 16)
            sp.dma_start(row[0:1, 2 * JP:2 * JP + 1], g_xattn.rearrange("(a b) -> a b", a=1)).then_inc(small_in, 16)
            sp.dma_start(row[0:1, 2 * JP + 1:2 * JP + 2], g_ffn.rearrange("(a b) -> a b", a=1)).then_inc(small_in, 16)
            sp.dma_start(mrow[0:1, :], mask.rearrange("b (a j) -> a (b j)", a=1)).then_inc(mask_in, 16)
            sp.dma_start(wr_raw[:], w_router.rearrange("(k p) e -> p k e", p=P)).then_inc(sm2_in, 16)
            with nc.allow_non_contiguous_dma("256 biases, one to a partition"):
                sp.dma_start(bcol[:], bvec.rearrange("(t p) -> p t", p=P)).then_inc(sm2_in, 16)
            after(sp, "const_z", 1)
            sp.dma_start(xn[0:J, 0:B, :], ctx_in.rearrange("b j d -> j b d")).then_inc(y_in, 16)
            for g in range(1, NG):
                sp.dma_start(acc[:, GT * g:GT * g + GT, :], x_v[:, GT * g:GT * g + GT, :]).then_inc(x_in[g], 16)

            def chunk(c, slot_, src):
                after(sp, "chunk_l", c - 1)
                sp.dma_start(stage[:, slot_, :], src).then_inc(stage_in[slot_], 16)

            after(sp, "wt_ps", 1)
            gv, uv = (a.rearrange("(k p) f -> k p f", p=P) for a in (gate_w, up_w))
            dv = down_w.rearrange("(c k p) d -> c p k d", p=P, k=2)
            for c, src in enumerate([gv[0], gv[1], uv[0], uv[1]]):
                chunk(c, c % 2, src)
            for c in range(2):
                after(sp, "chunk_l", 4 + c - 1)
                sp.dma_start(stage[:, c, :].rearrange("p (k d) -> p k d", k=2), dv[c]).then_inc(stage_in[c], 16)
            f1 = fc1.rearrange("e (k p) n -> (e k) p n", p=P)
            f2 = fc2.rearrange("e (k p) n -> e p k n", p=P)
            with sp.Fori(0, E // 2) as e2:
                for i in range(6):
                    sp.wait_ge(s["chunk_l"], 6 + 6 * e2 + i - 1)
                    e_i, part = i // 3, i % 3
                    if part < 2:
                        src = f1[bass.ds(e2 * 4 + 2 * e_i + part, 1)].rearrange("a p n -> p (a n)")
                        sp.dma_start(stage[:, i % 2, :], src).then_inc(stage_in[i % 2], 16)
                    else:
                        src = f2[bass.ds(e2 * 2 + e_i, 1)].rearrange("a p k n -> p (a k) n")
                        sp.dma_start(stage[:, i % 2, :].rearrange("p (k d) -> p k d", k=2), src).then_inc(stage_in[i % 2], 16)

            after(sp, "pad_rows", 3)
            sp.dma_start(rows[PAD_ROW:PAD_ROW + P, :], pad_rows).then_inc(s["pads"], 16)
            after(sp, "tb", 2)
            for e in range(E):
                c = sp.value_load(cnti[0:1, 0, e:e + 1], min_val=0, max_val=TOK)
                sp.dma_start(rows[bass.ds(c + e * REGION, P), :], pad_rows).then_inc(s["pads"], 16)
            after(sp, "pads", 16 * (E + 1))
            after(sp, "scattered", 16 * 2 * NT)
            after(sp, "tiles_known", 2)

            def load_tile(t, p):
                after(sp, "xT_ps", t - 1)
                after(sp, "dst_f", t - 1)
                off = sp.value_load(t_off[0:1, bass.ds(t, 1)], min_val=0, max_val=PAD_ROW)
                sp.dma_start(hr[:, p, :], rows[bass.ds(off, P), :]).then_inc(tile_in[p], 16)

            load_tile(0, 0)
            load_tile(1, 1)
            with sp.Fori(1, N_TILES // 2) as u:
                for p in range(2):
                    load_tile(2 * u + p, p)
            load_tile(N_TILES - 1, 0)

            sp.wait_ge(part_out[0], 16 * ((N_TILES + 1) // 2))
            sp.wait_ge(part_out[1], 16 * (N_TILES // 2))
            for g in range(NG):
                a, b = part_buf(g)
                if g >= 2:
                    after(sp, "done", g - 1)
                sp.dma_start(a, parts_v[0, :, GT * g:GT * g + GT, :]).then_inc(part_in[g], 16)
                sp.dma_start(b, parts_v[1, :, GT * g:GT * g + GT, :]).then_inc(part_in[g], 16)
            after(sp, "outs", 16 * NG)

        @block.gpsimd
        def _(pool):
            pool.memset(xn[:, 0:B, :], 0.0).then_inc(s["const_z"], 1)
            pool.memset(ident[:], 0.0).then_inc(s["const_v"], 1)
            pool.wait_ge(s["const_v"], 1)
            pool.affine_select(out=ident[:], in_=ident[:], compare_op=ALU.not_equal, fill=1.0, base=0,
                               pattern=[[-1, P]], channel_multiplier=1).then_inc(s["const_v"], 1)
            pool.memset(ones_row, 1.0).then_inc(s["const_v"], 1)
            pool.memset(row[0:1, 0:2 * JP], -BIG).then_inc(s["const_v"], 1)
            pool.memset(half[:], -0.5).then_inc(s["const_v"], 1)

            def rstd(ve, mv, rs, n, pw):
                pool.tensor_scalar(ve, mv, EPS, None, ALU.add).then_inc(s[pw], 1)
                pool.wait_ge(s[pw], n)
                h = half[:, 0:GT]
                return pool.tensor_tensor(out=rs, in0=ve, in1=h, op=ALU.pow)

            pool.wait_ge(s["const_v"], 5)

            def rstd_first(g):
                pool.wait_ge(s["mean1"], g + 1)
                sl = slice(GT * g, GT * g + GT)
                rstd(ve1[:, sl], mv1[:, sl, 1], rs1[:, sl], g + 1, "pow1").then_inc(s["rstd1"], 1)

            rstd_first(0)
            pool.memset(ones[:], 1.0).then_inc(s["const_v"], 1)
            pool.wait_ge(s["const_v"], 6)
            pool.affine_select(out=before[:], in_=ones[:], compare_op=ALU.is_gt, fill=0.0, base=0,
                               pattern=[[1, P]], channel_multiplier=-1).then_inc(s["const_v"], 1)
            for t_, step_, n_, base_, by_row in ((e_m8, 1, E, -E, 0), (e_reg, REGION, E, 0, 0), (tokf, P, NT, 0, 1),
                                                 (tix, 1, N_TILES, 0, 0), (e9, 1, E + 1, 0, 0)):
                pool.iota(t_[:], pattern=[[step_, n_]], base=base_, channel_multiplier=by_row,
                          allow_small_or_imprecise_dtypes=True).then_inc(s["const_p"], 1)
            pool.memset(seen[:, 0, :], 0.0).then_inc(s["const_p"], 1)

            def cut_lo(n, slot_, hi, lo):
                pool.wait_ge(s["chunk_h"], n)
                pool.tensor_tensor(out=lo, in0=stage[:, slot_, :], in1=hi.bitcast(F32), op=ALU.subtract)\
                    .then_inc(s["chunk_l"], 1)

            def second_norm(g):
                apart(pool, "mean2", g + 1)
                rstd(ve2[:], mv2[:, :, 1], rs2[:], g + 1, "pow2").then_inc(s["rstd2"], 1)

            def scatter(g, k):
                apart(pool, "slots", g + 1)
                for j in range(GT):
                    pool.indirect_dma_start(
                        out=rows, out_offset=bass.IndirectOffsetOnAxis(ap=slot[:, k, j:j + 1], axis=0),
                        in_=hr[:, j, :], in_offset=None, bounds_check=PAD_ROW - 1, oob_is_err=False,
                    ).then_inc(s["scattered"], 16)

            for c in range(3):
                cut_lo(c + 1, c % 2, sw_hi[:, c, :], sw_lo[:, c, :])
            for g in range(1, NG):
                rstd_first(g)
            for c in range(3, 6):
                cut_lo(c + 1, c % 2, sw_hi[:, c, :], sw_lo[:, c, :])
            second_norm(0)
            with pool.Fori(1, NG) as g:
                for i in range(CPI):
                    c = (g - 1) * CPI + i
                    cut_lo(6 + (g - 1) * CPI + i + 1, i % 2, at(ew_hi, c), at(ew_lo, c))
                    if i in (1, 3):
                        scatter(g - 1, i // 2)
                    if i == 5:
                        second_norm(g)
            for k in range(2):
                scatter(NG - 1, k)
            pool.memset(pad_rows[:, 0:D], 0.0).then_inc(s["pad_rows"], 1)
            pool.memset(pad_rows[:, D:D + 1], NOWHERE).then_inc(s["pad_rows"], 1)
            pool.memset(pad_rows[:, D + 1:ROW], 0.0).then_inc(s["pad_rows"], 1)

            def scatter_parts(n, p):
                after(pool, "dst_i", n)
                apart(pool, "y_sb", n)
                pool.indirect_dma_start(
                    out=parts, out_offset=bass.IndirectOffsetOnAxis(ap=dst[p][:, 0:1], axis=0),
                    in_=xp[:, p, 0:D], in_offset=None, bounds_check=2 * TOK - 1, oob_is_err=False,
                ).then_inc(part_out[p], 16)

            with pool.Fori(0, N_TILES // 2) as u:
                for p in range(2):
                    scatter_parts(2 * u + p + 1, p)
            scatter_parts(N_TILES, 0)

        @block.scalar
        def _(a):
            def hi(out_, in_, name):
                return a.activation(out_, in_, ACT.Identity).then_inc(s[name], 1)

            after(a, "wt_ps", 1)
            hi(wt_hi[:], bank[0][:], "wt_h")
            a.wait_ge(y_in, 16)
            hi(y_hi[:], xn[0:JP, 0:B, :], "y_h")
            after(a, "yT_ps", 1)
            hi(xp_hi[:, 0, 0:K * B * JP], bank[1][:, 0:K * B * JP], "yT_h")
            a.wait_ge(sm2_in, 32)
            hi(wr_hi[:], wr_raw[:], "wr_h")
            after(a, "yp_ps", 1)
            for o in range(K):
                a.activation(xp[:, 0, o * B * JP:(o + 1) * B * JP], bank[2][:, o * B * JP:(o + 1) * B * JP],
                             ACT.Relu, bias=bcol[:, o:o + 1]).then_inc(s["yp_r"], 1)
            a.wait_ge(s["yp_r"], K)
            hi(yp_hi[:], xp[:, 0, 0:K * B * JP], "yp_h")
            after(a, "row_ps", 1)
            a.activation(tg[:], bank[3][:, 2 * JP:2 * JP + 2], ACT.Tanh).then_inc(s["row_bc"], 1)

            def cut_hi(n, slot_, out_, turns):
                a.wait_ge(stage_in[slot_], 16 * turns)
                hi(out_, stage[:, slot_, :], "chunk_h")

            def turn_x(g):
                for k in range(K):
                    after(a, "xt_ps", K * g + k + 1)
                    after(a, "mt_ps", 2 * g)
                    hi(xt_hi[:, k, :], bank[k][:], "xt_h")

            def project(g):
                for o in range(K):
                    after(a, "xp_ps", K * g + o + 1)
                    after(a, "sc_ps", g)
                    after(a, "xp_l", K * g)
                    a.activation(xp[:, o, :], bank[2 + o][:], ACT.Relu, bias=bcol[:, o:o + 1]).then_inc(s["xp_r"], 1)
                    a.activation(xp_hi[:, o, :], bank[2 + o][:], ACT.Relu, bias=bcol[:, o:o + 1]).then_inc(s["xp_h"], 1)

            def softmax_exp(g):
                after(a, "sc_sub", g + 1)
                after(a, "eT_ps", g)
                a.activation(s_exp[:], s_in[:], ACT.Exp).then_inc(s["sc_exp"], 1)

            def turn_e(g):
                after(a, "eT_ps", g + 1)
                hi(xt_hi[0:JP, 0, :], bank[1][0:JP, :], "eT_h")

            def turn_h(g):
                for k in range(K):
                    after(a, "hT_ps", K * g + k + 1)
                    hi(ht_hi[:, k, :], bank[k][:], "hT_h")

            def silu(g, f):
                n = FC * g + f
                after(a, "gu_ps", n + 1)
                after(a, "act_l", n - 1)
                a.activation(act[:, f % 2, :], BG[:], ACT.Silu).then_inc(s["sil"], 1)

            def silu_hi(g, f):
                n = FC * g + f
                after(a, "prod", n + 1)
                after(a, "dn_ps", n - 1)
                hi(act_hi[:, f % 2, :], act[:, f % 2, :], "act_h")

            turn_x(0)
            for c in range(3):
                cut_hi(c + 1, c % 2, sw_hi[:, c, :], c // 2 + 1)
            project(0)
            softmax_exp(0)
            turn_e(0)
            for c in range(3, 6):
                cut_hi(c + 1, c % 2, sw_hi[:, c, :], c // 2 + 1)
            turn_h(0)
            with a.Fori(1, NG) as g:
                def chunks(lo_, hi_):
                    for i in range(lo_, hi_):
                        cut_hi(0, i % 2, at(ew_hi, (g - 1) * CPI + i), 3 + (g - 1) * (CPI // 2) + i // 2 + 1)
                silu(g - 1, 0)
                silu_hi(g - 1, 0)
                turn_x(g)
                chunks(0, 2)
                silu(g - 1, 1)
                silu_hi(g - 1, 1)
                project(g)
                chunks(2, 4)
                softmax_exp(g)
                silu(g - 1, 2)
                silu_hi(g - 1, 2)
                turn_e(g)
                chunks(4, 6)
                silu(g - 1, 3)
                silu_hi(g - 1, 3)
                chunks(6, 8)
                turn_h(g)
            for f in range(FC):
                silu(NG - 1, f)
                silu_hi(NG - 1, f)

            after(a, "weights_w", 1)
            a.activation(wsm[:, 1, :], wsm[:, 0, :], ACT.Tanh, scale=0.5).then_inc(s["w_tanh"], 1)

            def m_x(t, p):
                after(a, "xT_ps", t + 1)
                after(a, "h1_ps", t - 1)
                hi(xt_hi[:, p, 0:D], bank[2 + p][:, 0:D], "xT_h")

            def m_silu(t, p):
                after(a, "h1_ps", t + 1)
                after(a, "aT_ps", t - 1)
                a.activation(act[:, p, 0:I], bank[p][:, 0:I], ACT.Silu).then_inc(s["m_sil"], 1)

            def m_a(t, p):
                after(a, "aT_ps", t + 1)
                after(a, "y2_ps", t - 1)
                hi(xp_hi[:, p, 0:I], bank[4 + p][:, 0:I], "aT_h")

            def m_y(t, p, turns):
                after(a, "y2_ps", t + 1)
                if not (isinstance(turns, int) and turns == 0):
                    a.wait_ge(part_out[p], 16 * turns)
                a.activation(xp[:, p, 0:D], bank[6 + p][:, 0:D], ACT.Identity).then_inc(s["y_sb"], 1)

            a.wait_ge(s["xp_l"], K * NG)
            m_x(0, 0)
            m_x(1, 1)
            m_silu(0, 0)
            m_x(2, 0)
            m_silu(1, 1)
            m_a(0, 0)
            m_x(3, 1)
            full = (N_TILES - 4) // 2
            def step(t, p, turns, x_=True):
                m_silu(t, p)
                m_a(t - 1, 1 - p)
                if x_:
                    m_x(t + 2, p)
                m_y(t - 2, p, turns)
            step(2, 0, 0)
            step(3, 1, 0)
            with a.Fori(2, full + 1) as u:
                step(2 * u, 0, u - 1)
                step(2 * u + 1, 1, u - 1)
            t0 = 2 * (full + 1)
            for t in range(t0, N_TILES):
                step(t, t % 2, (t - 2) // 2, t + 2 < N_TILES)
            m_a(N_TILES - 1, (N_TILES - 1) % 2)
            for t in (N_TILES - 2, N_TILES - 1):
                m_y(t, t % 2, t // 2)

            for g in range(NG):
                after(a, "done", g + 1)
                a.dma_start(out_v[:, GT * g:GT * g + GT, :], acc[:, GT * g:GT * g + GT, :]).then_inc(s["outs"], 16)

        @block.vector
        def _(v):
            TT, TS = v.tensor_tensor, v.tensor_scalar
            give(v, "act_l", "prod", "dn_added")

            def lo(out_, in_, hi_, name):
                return TT(out_, in_, hi_.bitcast(F32), ALU.subtract).then_inc(s[name], 1)

            def stats_first(g):
                v.wait_ge(x_in[g], 16)
                for j in range(GT):
                    ins = v.bn_stats(st1[:, GT * g + j, :], acc[:, GT * g + j, :])
                ins.then_inc(s["stats1"], 1)
                v.wait_ge(s["stats1"], g + 1)
                for j in range(GT):
                    ins = v.bn_aggr(mv1[:, GT * g + j, :], st1[:, GT * g + j, :])
                ins.then_inc(s["mean1"], 1)

            def norm_first(g):
                after(v, "rstd1", g + 1 if isinstance(g, int) else NG)
                after(v, "xt_ps", K * g)
                for j in range(GT):
                    ins = TS(xn[:, j, :], at(acc, GT * g + j), at(mv1, GT * g + j)[:, 0:1],
                             rs1[:, bass.ds(GT * g + j, 1)], ALU.subtract, ALU.mult)
                ins.then_inc(s["xn_ready"], 1)

            stats_first(0)
            v.wait_ge(mask_in, 16)
            v.wait_ge(s["const_v"], 5)
            v.wait_ge(small_in, 32)
            TS(row[0:1, 0:2 * JP].rearrange("p (b j) -> p b j", b=B)[:, :, 0:J],
               mrow[0:1, :].rearrange("p (b j) -> p b j", b=B), -BIG, None, ALU.mult).then_inc(s["row_built"], 1)
            after(v, "wt_h", 1)
            lo(wt_lo[:], bank[0][:], wt_hi[:].rearrange("p k d -> p (k d)"), "wt_l")
            after(v, "y_h", 1)
            lo(y_lo[:], xn[0:JP, 0:B, :], y_hi[:], "y_l")
            after(v, "yT_h", 1)
            n = K * B * JP
            lo(xp_lo[:, 0, 0:n], bank[1][:, 0:n], xp_hi[:, 0, 0:n], "yT_l")
            after(v, "wr_h", 1)
            lo(wr_lo[:], wr_raw[:], wr_hi[:], "wr_l")
            after(v, "yp_h", 1)
            lo(yp_lo[:], xp[:, 0, 0:n], yp_hi[:].rearrange("p k b j -> p (k b j)"), "yp_l")
            after(v, "row_bc", 1)
            v.tensor_copy(mbias[:], bank[3][:, 0:2 * JP]).then_inc(s["row_bc"], 1)

            def turn_x(g):
                for k in range(K):
                    after(v, "xt_h", K * g + k + 1)
                    lo(xt_lo[:, k, :], bank[k][:], xt_hi[:, k, :], "xt_l")

            def project(g):
                for o in range(K):
                    after(v, "xp_h", K * g + o + 1)
                    lo(xp_lo[:, o, :], xp[:, o, :], xp_hi[:, o, :], "xp_l")

            def batch_of(g):
                return g // (NG // B)

            def softmax_in(g):
                after(v, "sc_ps", g + 1)
                after(v, "sc_exp", g)
                mb = bc_mid(at(mbias, batch_of(g)), GT)
                TT(s_in[:], bank[0][:, 0:GT * JP].rearrange("p (t j) -> p t j", t=GT), mb, ALU.add)\
                    .then_inc(s["sc_in"], 1)
                after(v, "sc_in", g + 1)
                v.tensor_reduce(s_max[:], s_in[:], X, ALU.max).then_inc(s["sc_max"], 1)
                after(v, "sc_max", g + 1)
                TT(s_in[:], s_in[:], bc_last(s_max[:], JP), ALU.subtract).then_inc(s["sc_sub"], 1)

            def softmax_out(g):
                after(v, "sc_exp", g + 1)
                v.tensor_reduce(s_sum[:], s_exp[:], X, ALU.add).then_inc(s["sc_sum"], 1)
                after(v, "sc_sum", g + 1)
                v.reciprocal(s_inv[:], s_sum[:]).then_inc(s["sc_inv"], 1)
                after(v, "sc_inv", g + 1)
                TS(s_coef[:], s_inv[:], tg[:, 0:1], None, ALU.mult).then_inc(s["sc_coef"], 1)

            def turn_e(g):
                after(v, "eT_h", g + 1)
                lo(xt_lo[0:JP, 0, :], bank[1][0:JP, :], xt_hi[0:JP, 0, :], "eT_l")

            def residual(g):
                after(v, "sc_coef", g + 1)
                for j in range(GT):
                    after(v, "mt_ps", 2 * g + j // 2 + 1)
                    a_j = at(acc, GT * g + j)
                    v.scalar_tensor_tensor(out=a_j, in0=bank[2 + j // 2][:, (j % 2) * D:(j % 2) * D + D],
                                           scalar=s_coef[:, j:j + 1], in1=a_j, op0=ALU.mult, op1=ALU.add)\
                        .then_inc(s["resid"], 1)
                for j in range(GT):
                    apart(v, "resid", GT * g + j + 1)
                    ins = v.bn_stats(st2[:, j, :], at(acc, GT * g + j))
                ins.then_inc(s["stats2"], 1)
                after(v, "rstd2", g)
                apart(v, "stats2", g + 1)
                for j in range(GT):
                    ins = v.bn_aggr(mv2[:, j, :], st2[:, j, :])
                ins.then_inc(s["mean2"], 1)

            def norm_second(g):
                after(v, "rstd2", g + 1)
                after(v, "scattered", 16 * 2 * GT * g)
                for j in range(GT):
                    ins = TS(hr[:, j, 0:D], at(acc, GT * g + j), mv2[:, j, 0:1], rs2[:, j:j + 1],
                             ALU.subtract, ALU.mult)
                ins.then_inc(s["h_ready"], 1)

            def turn_h(g):
                for k in range(K):
                    after(v, "hT_h", K * g + k + 1)
                    lo(ht_lo[:, k, :], bank[k][:], ht_hi[:, k, :], "hT_l")

            def route(g):
                n = [RT * g]

                def then(ins):
                    ins.then_inc(s["rt"], 1)
                    n[0] += 1
                    v.wait_ge(s["rt"], n[0])

                after(v, "lg_ps", g + 1)
                then(v.tensor_copy(lg[:], bank[2][:, 0:GT * E]))

                def top(k, logits, qa, qb, idx, oh):
                    m = mx[:, k, bass.ds(GT * g, GT)]
                    then(v.tensor_reduce(m, logits[:], X, ALU.max))
                    then(TT(qa[:], logits[:], bc_last(m, E), ALU.is_equal))
                    then(TT(qb[:], qa[:], bc_mid(e_m8[:], GT), ALU.mult))
                    then(v.tensor_reduce(idx[:], qb[:], X, ALU.min))
                    then(TT(oh[:], bc_mid(e_m8[:], GT), bc_last(idx[:], E), ALU.is_equal))

                top(0, lg, q1, q2, i1, oh1)
                then(v.scalar_tensor_tensor(out=lg2[:], in0=oh1[:], scalar=-BIG, in1=lg[:], op0=ALU.mult, op1=ALU.add))
                top(1, lg2, q1, q2, i2, oh2)
                then(TT(pick[:], oh1[:], oh2[:], ALU.add))
                for j in range(GT):
                    then(TT(at(seen, GT * g + j + 1), at(seen, GT * g + j), pick[:, j, :], ALU.add))
                v.tensor_copy(hr[:, :, D], tokf[:, bass.ds(GT * g, GT)]).then_inc(s["row_fields"], 1)
                TS(hr[:, :, D + 1], i1[:], float(E), None, ALU.add).then_inc(s["row_fields"], 1)

            def slots(g):
                n = [SL * g]

                def then(ins):
                    ins.then_inc(s["sl_step"], 1)
                    n[0] += 1
                    v.wait_ge(s["sl_step"], n[0])

                after(v, "rank_ps", g + 1)
                then(TT(place[:], bank[3][:, 0:GT * E].rearrange("p (t e) -> p t e", t=GT),
                        bc_mid(e_reg[:], GT), ALU.add))
                then(TT(q1[:], oh1[:], place[:], ALU.mult))
                then(TT(q2[:], oh2[:], place[:], ALU.mult))
                then(v.tensor_reduce(slotf[:, 0, :], q1[:], X, ALU.add))
                then(v.tensor_reduce(slotf[:, 1, :], q2[:], X, ALU.add))
                after(v, "row_fields", 2 * g + 2)
                v.tensor_copy(slot[:], slotf[:]).then_inc(s["slots"], 1)

            def product(g, f):
                n = FC * g + f
                after(v, "sil", n + 1)
                TT(act[:, f % 2, :], act[:, f % 2, :], BU[:], ALU.mult).then_inc(s["prod"], 1)

            def product_lo(g, f):
                n = FC * g + f
                after(v, "act_h", n + 1)
                lo(act_lo[:, f % 2, :], act[:, f % 2, :], act_hi[:, f % 2, :], "act_l")

            def add_down(g):
                after(v, "dn_ps", FC * g + FC)
                for j in range(GT):
                    a_j = at(acc, GT * g + j)
                    ins = v.scalar_tensor_tensor(out=a_j, in0=BD[j // 2][:, (j % 2) * D:(j % 2) * D + D],
                                                 scalar=tg[:, 1:2], in1=a_j, op0=ALU.mult, op1=ALU.add)
                ins.then_inc(s["dn_added"], 1)

            v.wait_ge(s["const_p"], N_CONST)
            norm_first(0)
            turn_x(0)
            for g in range(1, NG):
                stats_first(g)
            project(0)
            softmax_in(0)
            softmax_out(0)
            turn_e(0)
            residual(0)
            norm_second(0)
            turn_h(0)
            route(0)
            with v.Fori(1, NG) as g:
                norm_first(g)
                slots(g - 1)
                product(g - 1, 0)
                product_lo(g - 1, 0)
                turn_x(g)
                product(g - 1, 1)
                product_lo(g - 1, 1)
                project(g)
                softmax_in(g)
                softmax_out(g)
                product(g - 1, 2)
                product_lo(g - 1, 2)
                turn_e(g)
                residual(g)
                norm_second(g)
                product(g - 1, 3)
                product_lo(g - 1, 3)
                turn_h(g)
                add_down(g - 1)
                route(g)

            slots(NG - 1)
            m = [0]

            def then(ins):
                ins.then_inc(s["tb"], 1)
                m[0] += 1
                v.wait_ge(s["tb"], m[0])

            after(v, "cnt_ps", 1)
            then(v.tensor_copy(cnt[:], bank[2][:, 0:E]))
            then(v.tensor_copy(cnti[:, 0, :], cnt[:]))
            then(TS(cnti[:, 1, :], cnt[:], float(P - 1), None, ALU.add))
            then(TS(cnti[:, 2, :], cnti[:, 1, :], 7, None, ALU.arith_shift_right))
            then(v.tensor_copy(cum[:, 0, 0:E], cnti[:, 2, :]))
            for i, d in enumerate((1, 2, 4)):
                then(v.tensor_copy(cum[:, i + 1, 0:d], cum[:, i, 0:d]))
                then(TT(cum[:, i + 1, d:E], cum[:, i, d:E], cum[:, i, 0:E - d], ALU.add))
            then(TT(cmp9[:, :, 0:E], bc_mid(cum[:, 3, 0:E], N_TILES), bc_last(tix[:], E), ALU.is_le))
            then(v.tensor_reduce(t_exp[:], cmp9[:, :, 0:E], X, ALU.add))
            TS(t_w[:], t_exp[:], float(E - 1), None, ALU.min).then_inc(s["tiles_known"], 1)
            then(TT(cum[:, 4, 0:E], cum[:, 3, 0:E], cum[:, 0, 0:E], ALU.subtract))
            then(v.scalar_tensor_tensor(out=cum[:, 2, 0:E], in0=cum[:, 4, 0:E], scalar=-float(P), in1=e_reg[:],
                                        op0=ALU.mult, op1=ALU.add))
            then(v.scalar_tensor_tensor(out=cmp9b[:, :, 0:E], in0=bc_last(tix[:], E), scalar=float(P),
                                        in1=bc_mid(cum[:, 2, 0:E], N_TILES), op0=ALU.mult, op1=ALU.add))
            then(v.memset(cmp9b[:, :, E], float(PAD_ROW)))
            then(TT(cmp9, bc_mid(e9[:], N_TILES), bc_last(t_exp[:], E + 1), ALU.is_equal))
            then(TT(cmp9b, cmp9b, cmp9, ALU.mult))
            then(v.tensor_reduce(t_offf[:], cmp9b, X, ALU.add))
            v.tensor_copy(t_off[:], t_offf[:]).then_inc(s["tiles_known"], 1)

            for f in range(FC):
                product(NG - 1, f)
                product_lo(NG - 1, f)
            add_down(NG - 1)

            n0 = [0]

            def thenw(ins):
                ins.then_inc(s["weights_w"], 1)
                n0[0] += 1
                v.wait_ge(s["weights_w"], n0[0])

            thenw(TT(wsm[:, 0, :], mx[:, 0, :], mx[:, 1, :], ALU.subtract))
            after(v, "w_tanh", 1)
            thenw(TS(wsm[:, 2, :], wsm[:, 1, :], 0.5, 0.5, ALU.mult, ALU.add))
            thenw(TS(wsm[:, 3, :], wsm[:, 1, :], -0.5, 0.5, ALU.mult, ALU.add))
            thenw(TS(wsm[:, 4, :], wsm[:, 2, :], tg[:, 1:2], None, ALU.mult))
            thenw(TS(wsm[:, 5, :], wsm[:, 3, :], tg[:, 1:2], None, ALU.mult))

            def m_x(t, p):
                after(v, "xT_h", t + 1)
                lo(xt_lo[:, p, 0:D], bank[2 + p][:, 0:D], xt_hi[:, p, 0:D], "xT_l")

            def m_dst(t, p, turns):
                v.wait_ge(tile_in[p], 16 * turns)
                TS(dst_tmp[:, bass.ds(t, 1)], hr[:, p, D + 1:ROW], t_exp[:, bass.ds(t, 1)], float(TOK),
                   ALU.is_equal, ALU.mult).then_inc(s["dst_t"], 1)
                after(v, "dst_t", t + 1)
                TT(dstf[:, bass.ds(t, 1)], dst_tmp[:, bass.ds(t, 1)], hr[:, p, D:D + 1], ALU.add)\
                    .then_inc(s["dst_f"], 1)

            def m_prod(t, p):
                after(v, "m_sil", t + 1)
                TT(act[:, p, 0:I], act[:, p, 0:I], bank[p][:, I:2 * I], ALU.mult).then_inc(s["m_prod"], 1)

            def m_a(t, p):
                after(v, "aT_h", t + 1)
                lo(xp_lo[:, p, 0:I], bank[4 + p][:, 0:I], xp_hi[:, p, 0:I], "aT_l")

            def m_index(t, p, turns):
                after(v, "dst_f", t + 1)
                if not (isinstance(turns, int) and turns == 0):
                    v.wait_ge(part_out[p], 16 * turns)
                v.tensor_copy(dst[p][:], dstf[:, bass.ds(t, 1)]).then_inc(s["dst_i"], 1)

            m_dst(0, 0, 1)
            m_x(0, 0)
            m_dst(1, 1, 1)
            m_x(1, 1)
            m_prod(0, 0)
            m_dst(2, 0, 2)
            m_x(2, 0)
            m_prod(1, 1)
            m_a(0, 0)
            m_dst(3, 1, 2)
            m_x(3, 1)
            full = (N_TILES - 4) // 2

            def step(t, p, turns, x_=True):
                m_prod(t, p)
                m_a(t - 1, 1 - p)
                if x_:
                    m_dst(t + 2, p, turns + 3)
                    m_x(t + 2, p)
                m_index(t - 2, p, turns)

            step(2, 0, 0)
            step(3, 1, 0)
            with v.Fori(2, full + 1) as u:
                step(2 * u, 0, u - 1)
                step(2 * u + 1, 1, u - 1)
            t0 = 2 * (full + 1)
            for t in range(t0, N_TILES):
                step(t, t % 2, (t - 2) // 2, t + 2 < N_TILES)
            m_a(N_TILES - 1, (N_TILES - 1) % 2)
            for t in (N_TILES - 2, N_TILES - 1):
                m_index(t, t % 2, t // 2)

            for g in range(NG):
                second, first = part_buf(g)
                v.wait_ge(part_in[g], 32)
                for j in range(GT):
                    a_j = acc[:, GT * g + j, :]
                    c = GT * g + j
                    v.scalar_tensor_tensor(out=a_j, in0=first[:, j, :], scalar=wsm[:, 4, c:c + 1], in1=a_j,
                                           op0=ALU.mult, op1=ALU.add).then_inc(s["comb"], 1)
                for j in range(GT):
                    a_j = acc[:, GT * g + j, :]
                    c = GT * g + j
                    v.wait_ge(s["comb"], GT * g + j + 1)
                    ins = v.scalar_tensor_tensor(out=a_j, in0=second[:, j, :], scalar=wsm[:, 5, c:c + 1], in1=a_j,
                                                 op0=ALU.mult, op1=ALU.add)
                ins.then_inc(s["done"], 1)

        @block.tensor
        def _(pe):
            both = lambda h, l, *ix: (h[ix], l[ix])
            full_ = slice(None)
            give(pe, "dn_ps")
            pe.wait_ge(s["const_v"], 5)
            pe.wait_ge(w_in, 16)
            wst = stage[:].rearrange("p k (o h) -> p (k o) h", h=D)
            for t in range(K):
                for k in range(K):
                    ins = pe.transpose(bank[0][:, k * D + t * P:k * D + t * P + P], wst[:, t, k * P:(k + 1) * P], ident[:])
            ins.then_inc(s["wt_ps"], 1)
            pe.wait_ge(y_in, 16)
            for k in range(K):
                for b in range(B):
                    o = (k * B + b) * JP
                    ins = pe.transpose(bank[1][:, o:o + JP], xn[0:JP, b, k * P:(k + 1) * P], ident[0:JP, 0:JP])
            ins.then_inc(s["yT_ps"], 1)
            after(pe, "row_built", 1)
            pe.matmul(bank[3][:, 0:2 * JP + 2], ones_row, row, start=True, stop=True).then_inc(s["row_ps"], 1)
            after(pe, "wt_l", 1)
            after(pe, "yT_l", 1)
            N = B * JP
            for o in range(K):
                ins = mm3(pe, bank[2][:, o * N:(o + 1) * N],
                          lambda k: both(wt_hi, wt_lo, full_, k, slice(o * P, o * P + P)),
                          lambda k: both(xp_hi, xp_lo, full_, 0, slice(k * N, k * N + N)), K)
            ins.then_inc(s["yp_ps"], 1)

            def turn_x(g):
                after(pe, "xn_ready", g + 1)
                after(pe, "hT_l", K * g)
                for k in range(K):
                    for j in range(GT):
                        ins = pe.transpose(bank[k][:, j * P:(j + 1) * P], xn[:, j, k * P:(k + 1) * P], ident[:])
                    ins.then_inc(s["xt_ps"], 1)

            def project(g):
                after(pe, "xt_l", K * g + K)
                after(pe, "slots", g)
                for o in range(K):
                    mm3(pe, bank[2 + o][:], lambda k: both(wt_hi, wt_lo, full_, k, slice(o * P, o * P + P)),
                        lambda k: both(xt_hi, xt_lo, full_, k), K).then_inc(s["xp_ps"], 1)

            def scores(g):
                after(pe, "xp_l", K * g + K)
                b = g // (NG // B)
                for j in range(GT):
                    ins = mm3(pe, bank[0][:, j * JP:(j + 1) * JP],
                              lambda k: both(xp_hi, xp_lo, full_, k, slice(j * P, j * P + P)),
                              lambda k: tuple(w[:, k, bass.ds(b, 1), :].rearrange("p a j -> p (a j)")
                                              for w in (yp_hi, yp_lo)), K)
                ins.then_inc(s["sc_ps"], 1)

            def turn_e(g):
                after(pe, "sc_exp", g + 1)
                for j in range(GT):
                    ins = pe.transpose(bank[1][0:JP, j * P:(j + 1) * P], s_exp[:, j, :], ident[:])
                ins.then_inc(s["eT_ps"], 1)

            def matched(g):
                after(pe, "eT_l", g + 1)
                b = g // (NG // B)
                for j in range(GT):
                    ins = mm3(pe, bank[2 + j // 2][:, (j % 2) * D:(j % 2) * D + D],
                              lambda k: both(xt_hi, xt_lo, slice(0, JP), 0, slice(j * P, j * P + P)),
                              lambda k: tuple(w[:, bass.ds(b, 1), :].rearrange("p a d -> p (a d)")
                                              for w in (y_hi, y_lo)), 1)
                    if j % 2:
                        ins.then_inc(s["mt_ps"], 1)

            def turn_h(g):
                after(pe, "h_ready", g + 1)
                for k in range(K):
                    for j in range(GT):
                        ins = pe.transpose(bank[k][:, j * P:(j + 1) * P], hr[:, j, k * P:(k + 1) * P], ident[:])
                    ins.then_inc(s["hT_ps"], 1)

            def router(g):
                after(pe, "hT_l", K * g + K)
                for j in range(GT):
                    ins = mm3(pe, bank[2][:, j * E:(j + 1) * E],
                              lambda k: both(ht_hi, ht_lo, full_, k, slice(j * P, j * P + P)),
                              lambda k: both(wr_hi, wr_lo, full_, k), K)
                ins.then_inc(s["lg_ps"], 1)

            def rank(g):
                after(pe, "rt", RT * g + RT)
                pe.matmul(bank[3][:, 0:GT * E], before[:], pick[:].rearrange("p t e -> p (t e)"), start=True, stop=False)
                pe.matmul(bank[3][:, 0:GT * E], ones[:],
                          seen[:, bass.ds(GT * g, GT), :].rearrange("p t e -> p (t e)"),
                          start=False, stop=True).then_inc(s["rank_ps"], 1)

            def gate_up(g, f):
                n = FC * g + f
                after(pe, "prod", n)
                after(pe, "hT_l", K * g + K)
                for ps, c in ((BG, 0), (BU, 2)):
                    ins = mm3(pe, ps[:], lambda k: both(sw_hi, sw_lo, full_, c + k, slice(f * P, f * P + P)),
                              lambda k: both(ht_hi, ht_lo, full_, k), K)
                ins.then_inc(s["gu_ps"], 1)

            def down(g, f):
                after(pe, "act_l", FC * g + f + 1)
                if f == 0:
                    after(pe, "dn_added", g)
                for j in range(GT):
                    ins = mm3(pe, BD[j // 2][:, (j % 2) * D:(j % 2) * D + D],
                              lambda k: both(act_hi, act_lo, full_, f % 2, slice(j * P, j * P + P)),
                              lambda k: both(sw_hi, sw_lo, full_, 4 + f // 2, slice((f % 2) * D, (f % 2) * D + D)),
                              1, first=f == 0 and j % 2 == 0, last=f == FC - 1, lone=False)
                ins.then_inc(s["dn_ps"], 1)

            after(pe, "yp_l", 1)
            after(pe, "row_bc", 2)
            after(pe, "y_l", 1)
            after(pe, "wr_l", 1)
            turn_x(0)
            project(0)
            scores(0)
            turn_e(0)
            matched(0)
            turn_h(0)
            router(0)
            after(pe, "chunk_l", 6)
            with pe.Fori(1, NG) as g:
                gate_up(g - 1, 0)
                rank(g - 1)
                turn_x(g)
                gate_up(g - 1, 1)
                project(g)
                down(g - 1, 0)
                down(g - 1, 1)
                scores(g)
                gate_up(g - 1, 2)
                turn_e(g)
                down(g - 1, 2)
                matched(g)
                gate_up(g - 1, 3)
                down(g - 1, 3)
                turn_h(g)
                router(g)
            rank(NG - 1)
            pe.matmul(bank[2][:, 0:E], ones[:], seen[:, NT, :], start=True, stop=True).then_inc(s["cnt_ps"], 1)
            for f in range(FC):
                gate_up(NG - 1, f)
                if f:
                    down(NG - 1, f - 1)
            down(NG - 1, FC - 1)

            def m_turn_x(t, p, turns):
                pe.wait_ge(tile_in[p], 16 * turns)
                after(pe, "xT_l", t - 1)
                for k in range(K):
                    ins = pe.transpose(bank[2 + p][:, k * P:(k + 1) * P], hr[:, p, k * P:(k + 1) * P], ident[:])
                ins.then_inc(s["xT_ps"], 1)

            def expert_of(t):
                return pe.value_load(t_w[0:1, bass.ds(t, 1)], min_val=0, max_val=E - 1)

            def weights(e, c, lo_, hi_):
                return tuple(at(w, 3 * e + c)[:, lo_:hi_] for w in (ew_hi, ew_lo))

            def m_up(t, p):
                e = expert_of(t)
                after(pe, "xT_l", t + 1)
                after(pe, "m_prod", t - 1)
                mm3(pe, bank[p][:], lambda k: both(xt_hi, xt_lo, full_, p, slice(k * P, k * P + P)),
                    lambda k: weights(e, k, 0, 512), K).then_inc(s["h1_ps"], 1)

            def m_turn_a(t, p):
                after(pe, "m_prod", t + 1)
                after(pe, "aT_l", t - 1)
                for k in range(K):
                    ins = pe.transpose(bank[4 + p][:, k * P:(k + 1) * P], act[:, p, k * P:(k + 1) * P], ident[:])
                ins.then_inc(s["aT_ps"], 1)

            def m_down(t, p):
                e = expert_of(t)
                after(pe, "aT_l", t + 1)
                after(pe, "y_sb", t - 1)
                mm3(pe, bank[6 + p][:, 0:D], lambda k: both(xp_hi, xp_lo, full_, p, slice(k * P, k * P + P)),
                    lambda k: weights(e, 2, k * D, k * D + D), K).then_inc(s["y2_ps"], 1)

            after(pe, "dn_added", NG)
            after(pe, "tiles_known", 1)
            after(pe, "chunk_l", 6 + WCH)
            m_turn_x(0, 0, 1)
            m_turn_x(1, 1, 1)
            m_up(0, 0)
            m_turn_x(2, 0, 2)
            m_up(1, 1)
            m_turn_a(0, 0)
            m_turn_x(3, 1, 2)
            full = (N_TILES - 4) // 2

            def step(t, p, turns, x_=True):
                m_up(t, p)
                m_turn_a(t - 1, 1 - p)
                if x_:
                    m_turn_x(t + 2, p, turns)
                m_down(t - 2, p)

            step(2, 0, 3)
            step(3, 1, 3)
            with pe.Fori(2, full + 1) as u:
                step(2 * u, 0, u + 2)
                step(2 * u + 1, 1, u + 2)
            t0 = 2 * (full + 1)
            for t in range(t0, N_TILES):
                step(t, t % 2, t // 2 + 2, t + 2 < N_TILES)
            m_turn_a(N_TILES - 1, (N_TILES - 1) % 2)
            for t in (N_TILES - 2, N_TILES - 1):
                m_down(t, t % 2)


_INS = ["x", "ctx_1024", "mask_BxS2_bk0", "g_xattn", "g_ffn", "L0_xattn_W", "L0_xattn_b", "L0_ffn_w_router",
        "L0_ffn_fc1_w", "L0_ffn_fc2_w", "L0_ffn_gate_w", "L0_ffn_up_w", "L0_ffn_down_w"]


def kernel(**inputs):
    import numpy as _np
    import concourse.bacc as _bacc
    from concourse import mybir as _mybir
    from concourse.bass_utils import run_bass_kernel_spmd as _run

    nc = _bacc.Bacc("TRN2", target_bir_lowering=False, num_devices=1)
    arrays, args = {}, []
    for name in _INS:
        a = _np.ascontiguousarray(inputs[name])
        arrays[f"in_{name}"] = a
        args.append(nc.dram_tensor(f"in_{name}", a.shape, _mybir.dt.from_np(a.dtype), kind="ExternalInput").ap())
    args.append(nc.dram_tensor("out_0", (2, 1024, 256), _mybir.dt.float32, kind="ExternalOutput").ap())
    build(nc, *args)
    r = _run(nc, [arrays], core_ids=[0])
    return r.results[0]["out_0"]
```

```python
import concourse.bass as bass
from concourse import mybir
from contextlib import ExitStack

F32 = mybir.dt.float32
F32R = mybir.dt.float32r
BF16 = mybir.dt.bfloat16
I32 = mybir.dt.int32
U8 = mybir.dt.uint8
ALU = mybir.AluOpType
ACT = mybir.ActivationFunctionType
X = mybir.AxisListType.X

P = 128
B, S, D = 2, 1024, 256
J, JP = 77, 80
E, I = 8, 256
F = 512
TOK = B * S
GT = 4
GN = GT * P
NG = TOK // GN
NT = TOK // P
K = D // P
FC = F // P
REGION = TOK + P
PAD_ROW = E * REGION
ROW = D + 2
N_TILES = (2 * TOK + E * (P - 1)) // P
NOWHERE = 1.0e6
BIG = 1.0e30
EPS = 1e-5
WCH = 3 * E
N_CONST = 6
RT = 13
SL = 8
UNROLL = 6
CPI = WCH // NG


def build(nc, x, ctx_in, mask, g_xattn, g_ffn, W, bvec, w_router, fc1, fc2, gate_w, up_w, down_w, out):
    rows = nc.dram_tensor("rows", [PAD_ROW + P, ROW], F32).ap()
    parts = nc.dram_tensor("parts", [2 * TOK, D], F32).ap()
    x_v = x.rearrange("b (t p) d -> p (b t) d", p=P)
    out_v = out.rearrange("b (t p) d -> p (b t) d", p=P)
    parts_v = parts.rearrange("(k t p) d -> k p t d", k=2, p=P)

    with ExitStack() as ctx:
        def sb(name, shape, dt=F32):
            return ctx.enter_context(nc.sbuf_tensor(name, shape, dt))

        def sem(name):
            return ctx.enter_context(nc.semaphore(name))

        ew_hi = sb("ew_hi", [P, WCH, 512], F32R)
        ew_lo = sb("ew_lo", [P, WCH, 512], F32R)
        sw_hi = sb("sw_hi", [P, 6, 512], F32R)
        sw_lo = sb("sw_lo", [P, 6, 512], F32R)
        wt_hi = sb("wt_hi", [P, K, D], F32R)
        wt_lo = sb("wt_lo", [P, K, D], F32R)
        y_hi = sb("y_hi", [JP, B, D], F32R)
        y_lo = sb("y_lo", [JP, B, D], F32R)
        yp_hi = sb("yp_hi", [P, K, B, JP], F32R)
        yp_lo = sb("yp_lo", [P, K, B, JP], F32R)
        wr_hi = sb("wr_hi", [P, K, E], F32R)
        wr_lo = sb("wr_lo", [P, K, E], F32R)
        acc = sb("acc", [P, NT, D])
        xn = sb("xn", [P, GT, D])
        hr = sb("hr", [P, GT, ROW])
        ht_hi = sb("ht_hi", [P, K, GN], F32R)
        ht_lo = sb("ht_lo", [P, K, GN], F32R)
        xt_hi = sb("xt_hi", [P, K, GN], F32R)
        xt_lo = sb("xt_lo", [P, K, GN], F32R)
        xp_hi = sb("xp_hi", [P, K, GN], F32R)
        xp_lo = sb("xp_lo", [P, K, GN], F32R)
        hn = sb("hn", [P, GT, D])
        act = sb("act", [P, 2, GN])
        act_hi = sb("act_hi", [P, 2, GN], F32R)
        act_lo = sb("act_lo", [P, 2, GN], F32R)
        stage = sb("stage", [P, 2, 512])
        s_in = sb("s_in", [P, GT, JP])
        s_exp = s_in
        ident = sb("ident", [P, P])
        ones = sb("ones", [P, P], BF16)
        before = sb("before", [P, P], BF16)
        row = act[0:1, 0, 0:2 * JP + 2]
        ones_row = act[0:1, 1, 0:P]
        mrow = sb("mrow", [1, B * J], U8)
        mbias = sb("mbias", [P, B, JP])
        tg = sb("tg", [P, 2])
        bcol = sb("bcol", [P, K])
        wr_raw = sb("wr_raw", [P, K, E])
        half = sb("half", [P, GT])
        st1 = sb("st1", [P, NT, 6])
        mv1 = sb("mv1", [P, NT, 2])
        rs1 = sb("rs1", [P, NT])
        st2 = sb("st2", [P, GT, 6])
        mv2 = sb("mv2", [P, GT, 2])
        rs2 = sb("rs2", [P, GT])
        ve1 = sb("ve1", [P, NT])
        ve2 = sb("ve2", [P, GT])
        s_max = sb("s_max", [P, GT])
        s_sum = sb("s_sum", [P, GT])
        s_inv = sb("s_inv", [P, GT])
        s_coef = sb("s_coef", [P, GT])
        lg = sb("lg", [P, GT, E])
        lg2 = sb("lg2", [P, GT, E])
        q1 = sb("q1", [P, GT, E])
        q2 = sb("q2", [P, GT, E])
        oh1 = sb("oh1", [P, GT, E])
        oh2 = sb("oh2", [P, GT, E])
        pick = sb("pick", [P, GT, E], BF16)
        i1 = sb("i1", [P, GT])
        i2 = sb("i2", [P, GT])
        i_low = sb("i_low", [P, GT])
        low_first = sb("low_first", [P, NT])
        mx = sb("mx", [P, 2, NT])
        seen = sb("seen", [P, E], BF16)
        seen_g = sb("seen_g", [P, E])
        place = sb("place", [P, GT, E])
        slotf = sb("slotf", [P, 2, GT])
        slot = sb("slot", [P, 2, GT], I32)
        e_m8 = sb("e_m8", [P, E])
        e_reg = sb("e_reg", [P, E])
        tokf = sb("tokf", [P, NT])
        wsm = sb("wsm", [P, 6, NT])
        cnt = sb("cnt", [P, E])
        cnti = sb("cnti", [P, 3, E], I32)
        cum = sb("cum", [P, 5, E + 1])
        tix = sb("tix", [P, N_TILES])
        e9 = sb("e9", [P, E + 1])
        n9 = N_TILES * (E + 1)
        xn_flat = xn[:].rearrange("p t d -> p (t d)")
        cmp9 = xn_flat[:, 0:n9].rearrange("p (t e) -> p t e", e=E + 1)
        cmp9b = xn_flat[:, n9:2 * n9].rearrange("p (t e) -> p t e", e=E + 1)
        pad_rows = xn_flat[:, 2 * n9:2 * n9 + ROW]
        lgT = xn_flat[0:E, 0:GN]
        t_exp = sb("t_exp", [P, N_TILES])
        t_w = sb("t_w", [P, N_TILES], I32)
        low_tiles = sb("low_tiles", [P, 3], I32)
        t_off = sb("t_off", [P, N_TILES], I32)
        t_offf = sb("t_offf", [P, N_TILES])
        dst_tmp = sb("dst_tmp", [P, N_TILES])
        dstf = sb("dstf", [P, N_TILES])
        dst = [sb(f"dst{i}", [P, 1], I32) for i in range(4)]

        bank = [ctx.enter_context(nc.psum_tensor(f"bank{i}", [P, 512], F32)) for i in range(8)]
        BG, BU, BD = bank[4], bank[5], bank[6:8]

        names = """const_z const_p const_v rstd1 rstd2 row_built
            wt_ps wt_h wt_l y_h y_l yT_ps yT_h yT_l yp_ps yp_r yp_h yp_l wr_h wr_l row_ps row_bc
            stats1 mean1 xn_ready xt_ps xt_h xt_l xp_ps xp_r xp_h xp_l
            sc_ps sc_in sc_max sc_sub sc_exp sc_sum sc_inv sc_coef eT_ps eT_h eT_l mt_ps resid
            stats2 mean2 h_ready rows_kept rows_free seen_ready place_read hT_ps hT_h hT_l lgT_ps lgT_sb lg_ps rt rank_ps slots row_fields scattered
            gu_ps sil prod act_h act_l dn_ps dn_added cnt_ps pads tb tiles_known weights_w
            xT_ps xT_h xT_l h1_ps m_sil m_prod aT_ps aT_h aT_l y2_ps y_sb dst_t dst_f dst_i
            done outs sl_step w_tanh low_added0 low_added1 low_added2 low_added3 pad_rows passed pow1 pow2 chunk_h chunk_l""".split()
        s = {n: sem(n) for n in names}
        x_in = [sem(f"x_in{g}") for g in range(NG)]
        w_in, y_in, small_in, mask_in, sm2_in = (sem(n) for n in ("w_in", "y_in", "small_in", "mask_in", "sm2_in"))
        stage_in = [sem(f"stage_in{i}") for i in range(2)]
        tile_in = [sem(f"tile_in{i}") for i in range(2)]
        part_out = [sem(f"part_out{i}") for i in range(2)]
        low_in = [sem(f"low_in{g}") for g in range(NG)]
        high_in = [sem(f"high_in{g}") for g in range(NG)]

        ahead = {"act_l": 2, "dn_ps": 2, "prod": 1, "dn_added": 1, "seen_ready": 1, "rows_free": 1}

        def give(eng, *which):
            for name in which:
                eng.sem_inc(s[name], ahead[name])

        def after(eng, name, value):
            if not (isinstance(value, int) and value <= 0):
                eng.wait_ge(s[name], value + ahead.get(name, 0))

        def apart(eng, name, value):
            after(eng, name, value)
            eng.sem_inc(s["passed"], 1)

        def bc_mid(ap, n):
            return ap.unsqueeze(1).broadcast_to([ap.shape[0], n, ap.shape[1]])

        def bc_last(ap, n):
            return ap.unsqueeze(2).broadcast_to([ap.shape[0], ap.shape[1], n])

        def at(t3, i):
            return t3[:, bass.ds(i, 1), :].rearrange("p a d -> p (a d)")

        def mm3(pe, ps, lhs, rhs, chunks, first=True, last=True, lone=True):
            n, total, ins = 0, 3 * chunks, None
            for k in range(chunks):
                (lh, ll), (rh, rl) = lhs(k), rhs(k)
                for a, b in ((lh, rh), (lh, rl), (ll, rh)):
                    ins = pe.matmul(ps, a, b, start=first and n == 0, stop=last and n == total - 1,
                                    skip_group_check=not lone)
                    n += 1
            return ins

        def part_bufs(g):
            n = GT * D
            low_buf = (sw_hi, sw_hi, sw_hi, sw_lo)[g]
            low, high = (b[:].rearrange("p c n -> p (c n)").bitcast(F32)[:, m * n:(m + 1) * n]
                         .rearrange("p (t d) -> p t d", d=D) for b, m in ((low_buf, g % 3), (ew_hi, g)))
            return low, high

        def turns_of_groups(eng, turn):
            turn(-1)
            turn(0)
            with eng.Fori(1, NG - 1) as g:
                turn(g)
            turn(NG - 1)

        def parts_of(g):
            known = isinstance(g, int)
            return not known or g >= 1, not known or g >= 0, not known or g < NG - 1

        def add_part(eng, g, part, j):
            c = GT * g + j
            return eng.scalar_tensor_tensor(out=acc[:, c, :], in0=part_bufs(g)[part][:, j, :],
                                            scalar=wsm[:, 4 + part, c:c + 1], in1=acc[:, c, :],
                                            op0=ALU.mult, op1=ALU.add)

        def add_low(eng, g):
            eng.wait_ge(low_in[g], 16)
            for j in range(GT):
                add_part(eng, g, 0, j).then_inc(s[f"low_added{g}"], 1)

        def part_slot(t, p):
            return 2 + p if isinstance(t, int) and t >= N_TILES - 2 else p

        def slot_free(eng, t, p, turns):
            if part_slot(t, p) == p and not (isinstance(turns, int) and turns == 0):
                eng.wait_ge(part_out[p], 16 * turns)

        block = ctx.enter_context(nc.Block())

        @block.sync
        def _(sp):
            sp.dma_start(acc[:, 0:GT, :], x_v[:, 0:GT, :]).then_inc(x_in[0], 16)
            sp.dma_start(stage[:, :, :].rearrange("p k (o h) -> p (k o) h", h=D)[:, 0:K, :],
                         W.rearrange("(t p) h -> p t h", p=P)).then_inc(w_in, 16)
            sp.dma_start(row[0:1, 2 * JP:2 * JP + 1], g_xattn.rearrange("(a b) -> a b", a=1)).then_inc(small_in, 16)
            sp.dma_start(row[0:1, 2 * JP + 1:2 * JP + 2], g_ffn.rearrange("(a b) -> a b", a=1)).then_inc(small_in, 16)
            sp.dma_start(mrow[0:1, :], mask.rearrange("b (a j) -> a (b j)", a=1)).then_inc(mask_in, 16)
            sp.dma_start(wr_raw[:], w_router.rearrange("(k p) e -> p k e", p=P)).then_inc(sm2_in, 16)
            with nc.allow_non_contiguous_dma("256 biases, one to a partition"):
                sp.dma_start(bcol[:], bvec.rearrange("(t p) -> p t", p=P)).then_inc(sm2_in, 16)
            after(sp, "const_z", 1)
            sp.dma_start(xn[0:J, 0:B, :], ctx_in.rearrange("b j d -> j b d")).then_inc(y_in, 16)
            for g in range(1, NG):
                sp.dma_start(acc[:, GT * g:GT * g + GT, :], x_v[:, GT * g:GT * g + GT, :]).then_inc(x_in[g], 16)

            def chunk(c, slot_, src):
                after(sp, "chunk_l", c - 1)
                sp.dma_start(stage[:, slot_, :], src).then_inc(stage_in[slot_], 16)

            after(sp, "wt_ps", 1)
            gv, uv = (a.rearrange("(k p) f -> k p f", p=P) for a in (gate_w, up_w))
            dv = down_w.rearrange("(c k p) d -> c p k d", p=P, k=2)
            for c, src in enumerate([gv[0], gv[1], uv[0], uv[1]]):
                chunk(c, c % 2, src)
            for c in range(2):
                after(sp, "chunk_l", 4 + c - 1)
                sp.dma_start(stage[:, c, :].rearrange("p (k d) -> p k d", k=2), dv[c]).then_inc(stage_in[c], 16)
            f1 = fc1.rearrange("e (k p) n -> (e k) p n", p=P)
            f2 = fc2.rearrange("e (k p) n -> e p k n", p=P)
            with sp.Fori(0, E // 2) as e2:
                for i in range(6):
                    sp.wait_ge(s["chunk_l"], 6 + 6 * e2 + i - 1)
                    e_i, part = i // 3, i % 3
                    if part < 2:
                        src = f1[bass.ds(e2 * 4 + 2 * e_i + part, 1)].rearrange("a p n -> p (a n)")
                        sp.dma_start(stage[:, i % 2, :], src).then_inc(stage_in[i % 2], 16)
                    else:
                        src = f2[bass.ds(e2 * 2 + e_i, 1)].rearrange("a p k n -> p (a k) n")
                        sp.dma_start(stage[:, i % 2, :].rearrange("p (k d) -> p k d", k=2), src).then_inc(stage_in[i % 2], 16)

            after(sp, "pad_rows", 3)
            sp.dma_start(rows[PAD_ROW:PAD_ROW + P, :], pad_rows).then_inc(s["pads"], 16)
            after(sp, "tb", 2)
            for e in range(E):
                c = sp.value_load(cnti[0:1, 0, e:e + 1], min_val=0, max_val=TOK)
                sp.dma_start(rows[bass.ds(c + e * REGION, P), :], pad_rows).then_inc(s["pads"], 16)
            after(sp, "pads", 16 * (E + 1))
            after(sp, "scattered", 16 * 2 * NT)
            after(sp, "tiles_known", 2)

            def load_tile(t, p):
                after(sp, "xT_ps", t - 1)
                after(sp, "dst_f", t - 1)
                off = sp.value_load(t_off[0:1, bass.ds(t, 1)], min_val=0, max_val=PAD_ROW)
                sp.dma_start(hr[:, p, :], rows[bass.ds(off, P), :]).then_inc(tile_in[p], 16)

            load_tile(0, 0)
            load_tile(1, 1)
            with sp.Fori(1, N_TILES // 2) as u:
                for p in range(2):
                    load_tile(2 * u + p, p)
            load_tile(N_TILES - 1, 0)

            after(sp, "dn_added", NG)
            n_low = [sp.value_load(low_tiles[0:1, 1 + p:2 + p], min_val=16 * TOK // P // 2, max_val=16 * N_TILES)
                     for p in range(2)]
            for p in range(2):
                sp.wait_ge(part_out[p], n_low[p])
            for g in range(NG):
                after(sp, "y_sb", N_TILES - NG - 1 + g)
                sp.dma_start(part_bufs(g)[0], parts_v[0, :, GT * g:GT * g + GT, :]).then_inc(low_in[g], 16)
            sp.wait_ge(part_out[0], 16 * ((N_TILES + 1) // 2))
            sp.wait_ge(part_out[1], 16 * (N_TILES // 2))
            for g in range(NG):
                sp.dma_start(part_bufs(g)[1], parts_v[1, :, GT * g:GT * g + GT, :]).then_inc(high_in[g], 16)
            after(sp, "outs", 16 * NG)

        @block.gpsimd
        def _(pool):
            pool.memset(xn[:, 0:B, :], 0.0).then_inc(s["const_z"], 1)
            pool.memset(ident[:], 0.0).then_inc(s["const_v"], 1)
            pool.wait_ge(s["const_v"], 1)
            pool.affine_select(out=ident[:], in_=ident[:], compare_op=ALU.not_equal, fill=1.0, base=0,
                               pattern=[[-1, P]], channel_multiplier=1).then_inc(s["const_v"], 1)
            pool.memset(ones_row, 1.0).then_inc(s["const_v"], 1)
            pool.memset(row[0:1, 0:2 * JP], -BIG).then_inc(s["const_v"], 1)
            pool.memset(half[:], -0.5).then_inc(s["const_v"], 1)

            def rstd(ve, mv, rs, n, pw):
                pool.tensor_scalar(ve, mv, EPS, None, ALU.add).then_inc(s[pw], 1)
                pool.wait_ge(s[pw], n)
                h = half[:, 0:GT]
                return pool.tensor_tensor(out=rs, in0=ve, in1=h, op=ALU.pow)

            pool.wait_ge(s["const_v"], 5)

            def rstd_first(g):
                pool.wait_ge(s["mean1"], g + 1)
                sl = slice(GT * g, GT * g + GT)
                rstd(ve1[:, sl], mv1[:, sl, 1], rs1[:, sl], g + 1, "pow1").then_inc(s["rstd1"], 1)

            rstd_first(0)
            pool.memset(ones[:], 1.0).then_inc(s["const_v"], 1)
            pool.wait_ge(s["const_v"], 6)
            pool.affine_select(out=before[:], in_=ones[:], compare_op=ALU.is_gt, fill=0.0, base=0,
                               pattern=[[1, P]], channel_multiplier=-1).then_inc(s["const_v"], 1)
            for t_, step_, n_, base_, by_row in ((e_m8, 1, E, -E, 0), (e_reg, REGION, E, 0, 0), (tokf, P, NT, 0, 1),
                                                 (tix, 1, N_TILES, 0, 0), (e9, 1, E + 1, 0, 0)):
                pool.iota(t_[:], pattern=[[step_, n_]], base=base_, channel_multiplier=by_row,
                          allow_small_or_imprecise_dtypes=True).then_inc(s["const_p"], 1)
            pool.memset(seen[:], 0.0).then_inc(s["const_p"], 1)

            def cut_lo(n, slot_, hi, lo):
                pool.wait_ge(s["chunk_h"], n)
                pool.tensor_tensor(out=lo, in0=stage[:, slot_, :], in1=hi.bitcast(F32), op=ALU.subtract)\
                    .then_inc(s["chunk_l"], 1)

            def second_norm(g):
                apart(pool, "mean2", g + 1)
                rstd(ve2[:], mv2[:, :, 1], rs2[:], g + 1, "pow2").then_inc(s["rstd2"], 1)

            def scatter(g, k, tiles=range(GT)):
                if k == 0 and 0 in tiles:
                    after(pool, "rows_kept", g + 1)
                    apart(pool, "slots", g + 1)
                for j in tiles:
                    pool.indirect_dma_start(
                        out=rows, out_offset=bass.IndirectOffsetOnAxis(ap=slot[:, k, j:j + 1], axis=0),
                        in_=hr[:, j, :], in_offset=None, bounds_check=PAD_ROW - 1, oob_is_err=False,
                    ).then_inc(s["scattered"], 16)

            give(pool, "rows_free")

            def turn(g):
                back, mid, ahead_ = parts_of(g)
                if not mid:
                    rstd_first(1)
                    for c in range(6):
                        cut_lo(c + 1, c % 2, sw_hi[:, c, :], sw_lo[:, c, :])
                    return

                def chunks(lo_, hi_):
                    for i in range(lo_, hi_):
                        c = g * CPI + i
                        cut_lo(6 + g * CPI + i + 1, i % 2, at(ew_hi, c), at(ew_lo, c))
                if back:
                    chunks(0, 1)
                second_norm(g)
                if not back:
                    for later in range(2, NG):
                        rstd_first(later)
                if back:
                    for i in range(4):
                        scatter(g - 1, i // 2, (2 * (i % 2), 2 * (i % 2) + 1))
                        chunks(i + 1, i + 2)
                    chunks(5, CPI)
                    pool.wait_ge(s["scattered"], 16 * 2 * GT * g)
                    pool.sem_inc(s["rows_free"], 1)
                else:
                    chunks(0, CPI)

            turns_of_groups(pool, turn)
            after(pool, "lg_ps", NG)
            pool.memset(pad_rows[:, 0:D], 0.0).then_inc(s["pad_rows"], 1)
            pool.memset(pad_rows[:, D:D + 1], NOWHERE).then_inc(s["pad_rows"], 1)
            pool.memset(pad_rows[:, D + 1:ROW], 0.0).then_inc(s["pad_rows"], 1)
            for k in range(2):
                scatter(NG - 1, k)

            def scatter_parts(t, p):
                i = part_slot(t, p)
                after(pool, "dst_i", t + 1)
                apart(pool, "y_sb", t + 1)
                pool.indirect_dma_start(
                    out=parts, out_offset=bass.IndirectOffsetOnAxis(ap=dst[i][:, 0:1], axis=0),
                    in_=hn[:, i, :], in_offset=None, bounds_check=2 * TOK - 1, oob_is_err=False,
                ).then_inc(part_out[p], 16)

            t0 = (N_TILES - 2) // 2 * 2
            with pool.Fori(0, t0 // 2) as u:
                for p in range(2):
                    scatter_parts(2 * u + p, p)
            for t in range(t0, N_TILES):
                scatter_parts(t, t % 2)

        @block.scalar
        def _(a):
            def hi(out_, in_, name):
                return a.activation(out_, in_, ACT.Identity).then_inc(s[name], 1)

            after(a, "wt_ps", 1)
            hi(wt_hi[:], bank[0][:], "wt_h")
            a.wait_ge(y_in, 16)
            hi(y_hi[:], xn[0:JP, 0:B, :], "y_h")
            after(a, "yT_ps", 1)
            hi(xp_hi[:, 0, 0:K * B * JP], bank[1][:, 0:K * B * JP], "yT_h")
            a.wait_ge(sm2_in, 32)
            hi(wr_hi[:], wr_raw[:], "wr_h")

            def cut_hi(n, slot_, out_, turns):
                a.wait_ge(stage_in[slot_], 16 * turns)
                hi(out_, stage[:, slot_, :], "chunk_h")

            def turn_x(g):
                for k in range(K):
                    after(a, "xt_ps", K * g + k + 1)
                    after(a, "mt_ps", 2 * g)
                    hi(xt_hi[:, k, :], bank[k][:], "xt_h")

            def project(g):
                for o in range(K):
                    after(a, "xp_ps", K * g + o + 1)
                    a.activation(bank[2 + o][:], bank[2 + o][:], ACT.Relu, bias=bcol[:, o:o + 1])\
                        .then_inc(s["xp_r"], 1)
                after(a, "sc_ps", g)
                for o in range(K):
                    after(a, "xp_r", K * g + o + 1)
                    hi(xp_hi[:, o, :], bank[2 + o][:], "xp_h")

            def keep_rows(g):
                after(a, "rows_free", g)
                after(a, "h_ready", g + 1)
                a.activation(hr[:, :, 0:D], hn[:], ACT.Identity).then_inc(s["rows_kept"], 1)

            def softmax_exp(g):
                after(a, "sc_sub", g + 1)
                after(a, "eT_ps", g)
                a.activation(s_exp[:], s_in[:], ACT.Exp).then_inc(s["sc_exp"], 1)

            def turn_e(g):
                after(a, "eT_ps", g + 1)
                hi(xt_hi[0:JP, 0, :], bank[1][0:JP, :], "eT_h")

            def turn_h(g):
                for k in range(K):
                    after(a, "hT_ps", K * g + k + 1)
                    hi(ht_hi[:, k, :], bank[1 + 2 * k][:], "hT_h")

            def router(g):
                after(a, "lgT_ps", g + 1)
                a.activation(lgT, bank[2][0:E, :], ACT.Identity).then_inc(s["lgT_sb"], 1)

            def silu(g, f):
                n = FC * g + f
                after(a, "gu_ps", n + 1)
                after(a, "act_l", n - 1)
                a.activation(act[:, f % 2, :], BG[:], ACT.Silu).then_inc(s["sil"], 1)

            def silu_hi(g, f):
                n = FC * g + f
                after(a, "prod", n + 1)
                after(a, "dn_ps", n - 1)
                hi(act_hi[:, f % 2, :], act[:, f % 2, :], "act_h")

            def projected_context():
                after(a, "yp_ps", 1)
                for o in range(K):
                    yp_o = bank[7][:, o * B * JP:(o + 1) * B * JP]
                    a.activation(yp_o, yp_o, ACT.Relu, bias=bcol[:, o:o + 1]).then_inc(s["yp_r"], 1)
                a.wait_ge(s["yp_r"], K)
                hi(yp_hi[:], bank[7][:, 0:K * B * JP], "yp_h")
                after(a, "row_ps", 1)
                a.activation(tg[:], bank[6][:, 2 * JP:2 * JP + 2], ACT.Tanh).then_inc(s["row_bc"], 1)

            def turn(g):
                back, mid, ahead_ = parts_of(g)

                def chunks(lo_, hi_):
                    for i in range(lo_, hi_):
                        cut_hi(0, i % 2, at(ew_hi, g * CPI + i), 3 + g * (CPI // 2) + i // 2 + 1)

                def shared_chunks(lo_, hi_):
                    for c in range(lo_, hi_):
                        cut_hi(c + 1, c % 2, sw_hi[:, c, :], c // 2 + 1)
                if back:
                    silu(g - 1, 0)
                    silu_hi(g - 1, 0)
                if ahead_:
                    turn_x(g + 1)
                if back:
                    keep_rows(g - 1)
                    chunks(0, 1)
                    silu(g - 1, 1)
                    chunks(1, 2)
                    silu_hi(g - 1, 1)
                if not mid:
                    projected_context()
                if ahead_:
                    project(g + 1)
                if not mid:
                    shared_chunks(0, 2)
                if back:
                    silu(g - 1, 2)
                    chunks(2, 3)
                    silu_hi(g - 1, 2)
                    chunks(3, 4)
                elif mid:
                    chunks(0, 4)
                if back:
                    silu(g - 1, 3)
                if ahead_:
                    softmax_exp(g + 1)
                if mid:
                    turn_h(g)
                if back:
                    silu_hi(g - 1, 3)
                if ahead_:
                    turn_e(g + 1)
                if mid:
                    router(g)
                    chunks(4, 6)
                else:
                    shared_chunks(2, 6)

            turns_of_groups(a, turn)
            keep_rows(NG - 1)
            for f in range(FC):
                silu(NG - 1, f)
                silu_hi(NG - 1, f)

            after(a, "weights_w", 3)
            a.activation(wsm[:, 1, :], wsm[:, 0, :], ACT.Tanh, scale=0.5).then_inc(s["w_tanh"], 1)

            def m_x(t, p):
                after(a, "xT_ps", t + 1)
                after(a, "h1_ps", t - 1)
                hi(xt_hi[:, p, 0:D], bank[2 + p][:, 0:D], "xT_h")

            def m_silu(t, p):
                after(a, "h1_ps", t + 1)
                after(a, "aT_ps", t - 1)
                a.activation(act[:, p, 0:I], bank[p][:, 0:I], ACT.Silu).then_inc(s["m_sil"], 1)

            def m_a(t, p):
                after(a, "aT_ps", t + 1)
                after(a, "y2_ps", t - 1)
                hi(xp_hi[:, p, 0:I], bank[4 + p][:, 0:I], "aT_h")

            def m_y(t, p, turns):
                after(a, "y2_ps", t + 1)
                slot_free(a, t, p, turns)
                a.activation(hn[:, part_slot(t, p), :], bank[6 + p][:, 0:D], ACT.Identity).then_inc(s["y_sb"], 1)

            a.wait_ge(s["xp_l"], K * NG)
            m_x(0, 0)
            m_x(1, 1)
            m_silu(0, 0)
            m_x(2, 0)
            m_silu(1, 1)
            m_a(0, 0)
            m_x(3, 1)
            full = (N_TILES - 4) // 2
            def step(t, p, turns, x_=True):
                m_silu(t, p)
                m_a(t - 1, 1 - p)
                if x_:
                    m_x(t + 2, p)
                m_y(t - 2, p, turns)
            step(2, 0, 0)
            step(3, 1, 0)
            with a.Fori(2, full + 1) as u:
                step(2 * u, 0, u - 1)
                step(2 * u + 1, 1, u - 1)
            t0 = 2 * (full + 1)
            for t in range(t0, N_TILES):
                step(t, t % 2, (t - 2) // 2, t + 2 < N_TILES)
            m_a(N_TILES - 1, (N_TILES - 1) % 2)
            for t in (N_TILES - 2, N_TILES - 1):
                m_y(t, t % 2, t // 2)

            for g in range(NG):
                after(a, "done", GT * g + GT)
                a.dma_start(out_v[:, GT * g:GT * g + GT, :], acc[:, GT * g:GT * g + GT, :]).then_inc(s["outs"], 16)

        @block.vector
        def _(v):
            TT, TS = v.tensor_tensor, v.tensor_scalar
            give(v, "act_l", "prod", "dn_added", "seen_ready")

            def lo(out_, in_, hi_, name):
                return TT(out_, in_, hi_.bitcast(F32), ALU.subtract).then_inc(s[name], 1)

            def stats_first(g):
                v.wait_ge(x_in[g], 16)
                for j in range(GT):
                    ins = v.bn_stats(st1[:, GT * g + j, :], acc[:, GT * g + j, :])
                ins.then_inc(s["stats1"], 1)
                v.wait_ge(s["stats1"], g + 1)
                for j in range(GT):
                    ins = v.bn_aggr(mv1[:, GT * g + j, :], st1[:, GT * g + j, :])
                ins.then_inc(s["mean1"], 1)

            def norm_first(g):
                after(v, "rstd1", g + 1 if isinstance(g, int) else NG)
                after(v, "xt_ps", K * g)
                after(v, "lg_ps", g - 1)
                for j in range(GT):
                    ins = TS(xn[:, j, :], at(acc, GT * g + j), at(mv1, GT * g + j)[:, 0:1],
                             rs1[:, bass.ds(GT * g + j, 1)], ALU.subtract, ALU.mult)
                ins.then_inc(s["xn_ready"], 1)

            stats_first(0)
            v.wait_ge(mask_in, 16)
            v.wait_ge(s["const_v"], 5)
            v.wait_ge(small_in, 32)
            TS(row[0:1, 0:2 * JP].rearrange("p (b j) -> p b j", b=B)[:, :, 0:J],
               mrow[0:1, :].rearrange("p (b j) -> p b j", b=B), -BIG, None, ALU.mult).then_inc(s["row_built"], 1)
            after(v, "wt_h", 1)
            lo(wt_lo[:], bank[0][:], wt_hi[:].rearrange("p k d -> p (k d)"), "wt_l")
            after(v, "y_h", 1)
            lo(y_lo[:], xn[0:JP, 0:B, :], y_hi[:], "y_l")
            after(v, "yT_h", 1)
            n = K * B * JP
            lo(xp_lo[:, 0, 0:n], bank[1][:, 0:n], xp_hi[:, 0, 0:n], "yT_l")
            after(v, "yT_ps", 1)
            after(v, "y_l", 1)
            norm_first(0)

            def projected_context():
                after(v, "yp_h", 1)
                lo(yp_lo[:], bank[7][:, 0:n], yp_hi[:].rearrange("p k b j -> p (k b j)"), "yp_l")
                after(v, "row_bc", 1)
                v.tensor_copy(mbias[:], bank[6][:, 0:2 * JP]).then_inc(s["row_bc"], 1)
                after(v, "wr_h", 1)
                lo(wr_lo[:], wr_raw[:], wr_hi[:], "wr_l")

            def turn_x(g):
                for k in range(K):
                    after(v, "xt_h", K * g + k + 1)
                    lo(xt_lo[:, k, :], bank[k][:], xt_hi[:, k, :], "xt_l")

            def project(g):
                for o in range(K):
                    after(v, "xp_h", K * g + o + 1)
                    lo(xp_lo[:, o, :], bank[2 + o][:], xp_hi[:, o, :], "xp_l")

            def batch_of(g):
                return g // (NG // B)

            def softmax_in(g):
                after(v, "sc_ps", g + 1)
                after(v, "sc_exp", g)
                mb = bc_mid(at(mbias, batch_of(g)), GT)
                TT(s_in[:], bank[0][:, 0:GT * JP].rearrange("p (t j) -> p t j", t=GT), mb, ALU.add)\
                    .then_inc(s["sc_in"], 1)
                after(v, "sc_in", g + 1)
                v.tensor_reduce(s_max[:], s_in[:], X, ALU.max).then_inc(s["sc_max"], 1)
                after(v, "sc_max", g + 1)
                TT(s_in[:], s_in[:], bc_last(s_max[:], JP), ALU.subtract).then_inc(s["sc_sub"], 1)

            def softmax_out(g):
                after(v, "sc_exp", g + 1)
                v.tensor_reduce(s_sum[:], s_exp[:], X, ALU.add).then_inc(s["sc_sum"], 1)
                after(v, "sc_sum", g + 1)
                v.reciprocal(s_inv[:], s_sum[:]).then_inc(s["sc_inv"], 1)
                after(v, "sc_inv", g + 1)
                TS(s_coef[:], s_inv[:], tg[:, 0:1], None, ALU.mult).then_inc(s["sc_coef"], 1)

            def turn_e(g):
                after(v, "eT_h", g + 1)
                lo(xt_lo[0:JP, 0, :], bank[1][0:JP, :], xt_hi[0:JP, 0, :], "eT_l")

            def residual(g):
                after(v, "sc_coef", g + 1)
                for j in range(GT):
                    after(v, "mt_ps", 2 * g + j // 2 + 1)
                    a_j = at(acc, GT * g + j)
                    v.scalar_tensor_tensor(out=a_j, in0=bank[2 + j // 2][:, (j % 2) * D:(j % 2) * D + D],
                                           scalar=s_coef[:, j:j + 1], in1=a_j, op0=ALU.mult, op1=ALU.add)\
                        .then_inc(s["resid"], 1)

            def stats_second(g):
                for j in range(GT):
                    apart(v, "resid", GT * g + j + 1)
                    ins = v.bn_stats(st2[:, j, :], at(acc, GT * g + j))
                ins.then_inc(s["stats2"], 1)
                after(v, "rstd2", g)
                apart(v, "stats2", g + 1)
                for j in range(GT):
                    ins = v.bn_aggr(mv2[:, j, :], st2[:, j, :])
                ins.then_inc(s["mean2"], 1)

            def norm_second(g):
                after(v, "rstd2", g + 1)
                after(v, "rows_kept", g)
                for j in range(GT):
                    ins = TS(hn[:, j, :], at(acc, GT * g + j), mv2[:, j, 0:1], rs2[:, j:j + 1],
                             ALU.subtract, ALU.mult)
                ins.then_inc(s["h_ready"], 1)

            def turn_h(g):
                for k in range(K):
                    after(v, "hT_h", K * g + k + 1)
                    lo(ht_lo[:, k, :], bank[1 + 2 * k][:], ht_hi[:, k, :], "hT_l")

            def route(g):
                n = [RT * g]

                def then(ins):
                    ins.then_inc(s["rt"], 1)
                    n[0] += 1
                    v.wait_ge(s["rt"], n[0])

                after(v, "lg_ps", g + 1)
                then(v.tensor_copy(lg[:], bank[2][:, 0:GT * E]))

                def top(k, logits, qa, qb, idx, oh):
                    m = mx[:, k, bass.ds(GT * g, GT)]
                    then(v.tensor_reduce(m, logits[:], X, ALU.max))
                    then(TT(qa[:], logits[:], bc_last(m, E), ALU.is_equal))
                    then(TT(qb[:], qa[:], bc_mid(e_m8[:], GT), ALU.mult))
                    then(v.tensor_reduce(idx[:], qb[:], X, ALU.min))
                    then(TT(oh[:], bc_mid(e_m8[:], GT), bc_last(idx[:], E), ALU.is_equal))

                top(0, lg, q1, q2, i1, oh1)
                then(v.scalar_tensor_tensor(out=lg2[:], in0=oh1[:], scalar=-BIG, in1=lg[:], op0=ALU.mult, op1=ALU.add))
                top(1, lg2, q1, q2, i2, oh2)
                then(TT(pick[:], oh1[:], oh2[:], ALU.add))

            def places(g):
                after(v, "rank_ps", g + 1)
                TT(place[:], bank[2][:, 0:GT * E].rearrange("p (t e) -> p t e", t=GT),
                   bc_mid(e_reg[:], GT), ALU.add).then_inc(s["place_read"], 1)

            def slots(g):
                n = [SL * g]

                def step(ins):
                    ins.then_inc(s["sl_step"], 1)
                    n[0] += 1

                def steps_done():
                    v.wait_ge(s["sl_step"], n[0])

                step(v.tensor_reduce(seen_g[:], pick[:].rearrange("p t e -> p e t"), X, ALU.add))
                step(TT(i_low[:], i1[:], i2[:], ALU.min))
                step(TT(low_first[:, bass.ds(GT * g, GT)], i1[:], i2[:], ALU.is_lt))
                after(v, "place_read", g + 1)
                step(TT(q1[:], oh1[:], place[:], ALU.mult))
                step(TT(q2[:], oh2[:], place[:], ALU.mult))
                steps_done()
                step(v.tensor_reduce(slotf[:, 0, :], q1[:], X, ALU.add))
                step(v.tensor_reduce(slotf[:, 1, :], q2[:], X, ALU.add))
                TT(seen[:], seen[:], seen_g[:], ALU.add).then_inc(s["seen_ready"], 1)
                after(v, "rows_free", g)
                step(v.tensor_copy(hr[:, :, D], tokf[:, bass.ds(GT * g, GT)]))
                steps_done()
                v.tensor_scalar(hr[:, :, D + 1], i_low[:], float(E), None, ALU.add).then_inc(s["row_fields"], 1)
                after(v, "row_fields", g + 1)
                v.tensor_copy(slot[:], slotf[:]).then_inc(s["slots"], 1)

            def product(g, f):
                n = FC * g + f
                after(v, "sil", n + 1)
                TT(act[:, f % 2, :], act[:, f % 2, :], BU[:], ALU.mult).then_inc(s["prod"], 1)

            def product_lo(g, f):
                n = FC * g + f
                after(v, "act_h", n + 1)
                lo(act_lo[:, f % 2, :], act[:, f % 2, :], act_hi[:, f % 2, :], "act_l")

            def add_down(g):
                after(v, "dn_ps", FC * g + FC)
                for j in range(GT):
                    a_j = at(acc, GT * g + j)
                    ins = v.scalar_tensor_tensor(out=a_j, in0=BD[j // 2][:, (j % 2) * D:(j % 2) * D + D],
                                                 scalar=tg[:, 1:2], in1=a_j, op0=ALU.mult, op1=ALU.add)
                ins.then_inc(s["dn_added"], 1)

            v.wait_ge(s["const_p"], N_CONST)
            def turn(g):
                back, mid, ahead_ = parts_of(g)
                if not isinstance(g, int):
                    norm_first(g + 1)
                if back:
                    route(g - 1)
                    product(g - 1, 0)
                if mid:
                    residual(g)
                if back:
                    product_lo(g - 1, 0)
                if ahead_:
                    turn_x(g + 1)
                if not mid:
                    projected_context()
                if back:
                    places(g - 1)
                    product(g - 1, 1)
                if mid:
                    stats_second(g)
                if back:
                    product_lo(g - 1, 1)
                    slots(g - 1)
                if mid:
                    norm_second(g)
                if ahead_:
                    project(g + 1)
                if back:
                    product(g - 1, 2)
                    product_lo(g - 1, 2)
                if not mid:
                    stats_first(1)
                    stats_first(2)
                    norm_first(1)
                if ahead_:
                    softmax_in(g + 1)
                if not mid:
                    for later in range(3, NG):
                        stats_first(later)
                if back:
                    product(g - 1, 3)
                if mid:
                    turn_h(g)
                if back:
                    product_lo(g - 1, 3)
                if ahead_:
                    turn_e(g + 1)
                    softmax_out(g + 1)
                if back and not (isinstance(g, int) and g == NG - 1):
                    add_down(g - 1)

            turns_of_groups(v, turn)
            route(NG - 1)
            product(NG - 1, 0)
            places(NG - 1)
            slots(NG - 1)
            add_down(NG - 2)
            product_lo(NG - 1, 0)
            m = [0]

            def then(ins):
                ins.then_inc(s["tb"], 1)
                m[0] += 1
                v.wait_ge(s["tb"], m[0])

            after(v, "cnt_ps", 1)
            then(v.tensor_copy(cnt[:], bank[3][:, 0:E]))
            then(v.tensor_copy(cnti[:, 0, :], cnt[:]))
            product(NG - 1, 1)
            product_lo(NG - 1, 1)
            then(TS(cnti[:, 1, :], cnt[:], float(P - 1), None, ALU.add))
            then(TS(cnti[:, 2, :], cnti[:, 1, :], 7, None, ALU.arith_shift_right))
            then(v.tensor_copy(cum[:, 0, 0:E], cnti[:, 2, :]))
            for i, d in enumerate((1, 2, 4)):
                then(v.tensor_copy(cum[:, i + 1, 0:d], cum[:, i, 0:d]))
                then(TT(cum[:, i + 1, d:E], cum[:, i, d:E], cum[:, i, 0:E - d], ALU.add))
            product(NG - 1, 2)
            then(v.tensor_copy(low_tiles[:, 0:1], cum[:, 3, E - 2:E - 1]))
            then(TS(low_tiles[:, 1:2], low_tiles[:, 0:1], 1, None, ALU.add))
            then(TS(low_tiles[:, 2:3], low_tiles[:, 0:1], 1, 4, ALU.arith_shift_right, ALU.logical_shift_left))
            then(TS(low_tiles[:, 1:2], low_tiles[:, 1:2], 1, 4, ALU.arith_shift_right, ALU.logical_shift_left))
            then(TT(cmp9[:, :, 0:E], bc_mid(cum[:, 3, 0:E], N_TILES), bc_last(tix[:], E), ALU.is_le))
            then(v.tensor_reduce(t_exp[:], cmp9[:, :, 0:E], X, ALU.add))
            TS(t_w[:], t_exp[:], float(E - 1), None, ALU.min).then_inc(s["tiles_known"], 1)
            then(TT(cum[:, 4, 0:E], cum[:, 3, 0:E], cum[:, 0, 0:E], ALU.subtract))
            then(v.scalar_tensor_tensor(out=cum[:, 2, 0:E], in0=cum[:, 4, 0:E], scalar=-float(P), in1=e_reg[:],
                                        op0=ALU.mult, op1=ALU.add))
            then(v.scalar_tensor_tensor(out=cmp9b[:, :, 0:E], in0=bc_last(tix[:], E), scalar=float(P),
                                        in1=bc_mid(cum[:, 2, 0:E], N_TILES), op0=ALU.mult, op1=ALU.add))
            then(v.memset(cmp9b[:, :, E], float(PAD_ROW)))
            then(TT(cmp9, bc_mid(e9[:], N_TILES), bc_last(t_exp[:], E + 1), ALU.is_equal))
            then(TT(cmp9b, cmp9b, cmp9, ALU.mult))
            then(v.tensor_reduce(t_offf[:], cmp9b, X, ALU.add))
            v.tensor_copy(t_off[:], t_offf[:]).then_inc(s["tiles_known"], 1)

            product_lo(NG - 1, 2)
            n0 = [0]

            def thenw(ins):
                ins.then_inc(s["weights_w"], 1)
                n0[0] += 1
                v.wait_ge(s["weights_w"], n0[0])

            v.wait_ge(s["sl_step"], SL * NG)
            thenw(TS(wsm[:, 2, :], low_first[:], 2.0, -1.0, ALU.mult, ALU.add))
            thenw(TT(wsm[:, 3, :], mx[:, 0, :], mx[:, 1, :], ALU.subtract))
            thenw(TT(wsm[:, 0, :], wsm[:, 2, :], wsm[:, 3, :], ALU.mult))
            product(NG - 1, 3)
            product_lo(NG - 1, 3)

            def m_x(t, p):
                after(v, "xT_h", t + 1)
                lo(xt_lo[:, p, 0:D], bank[2 + p][:, 0:D], xt_hi[:, p, 0:D], "xT_l")

            def m_dst(t, p, turns):
                v.wait_ge(tile_in[p], 16 * turns)
                TS(dst_tmp[:, bass.ds(t, 1)], hr[:, p, D + 1:ROW], t_exp[:, bass.ds(t, 1)], float(TOK),
                   ALU.not_equal, ALU.mult).then_inc(s["dst_t"], 1)
                after(v, "dst_t", t + 1)
                TT(dstf[:, bass.ds(t, 1)], dst_tmp[:, bass.ds(t, 1)], hr[:, p, D:D + 1], ALU.add)\
                    .then_inc(s["dst_f"], 1)

            def m_prod(t, p):
                after(v, "m_sil", t + 1)
                TT(act[:, p, 0:I], act[:, p, 0:I], bank[p][:, I:2 * I], ALU.mult).then_inc(s["m_prod"], 1)

            def m_a(t, p):
                after(v, "aT_h", t + 1)
                lo(xp_lo[:, p, 0:I], bank[4 + p][:, 0:I], xp_hi[:, p, 0:I], "aT_l")

            def m_index(t, p, turns):
                after(v, "dst_f", t + 1)
                slot_free(v, t, p, turns)
                v.tensor_copy(dst[part_slot(t, p)][:], dstf[:, bass.ds(t, 1)]).then_inc(s["dst_i"], 1)

            m_dst(0, 0, 1)
            m_x(0, 0)
            m_dst(1, 1, 1)
            m_x(1, 1)
            add_down(NG - 1)
            after(v, "w_tanh", 1)
            thenw(TS(wsm[:, 2, :], wsm[:, 1, :], 0.5, 0.5, ALU.mult, ALU.add))
            thenw(TS(wsm[:, 3, :], wsm[:, 1, :], -0.5, 0.5, ALU.mult, ALU.add))
            thenw(TS(wsm[:, 4, :], wsm[:, 2, :], tg[:, 1:2], None, ALU.mult))
            thenw(TS(wsm[:, 5, :], wsm[:, 3, :], tg[:, 1:2], None, ALU.mult))
            m_prod(0, 0)
            m_dst(2, 0, 2)
            m_x(2, 0)
            m_prod(1, 1)
            m_a(0, 0)
            m_dst(3, 1, 2)
            m_x(3, 1)
            full = (N_TILES - 4) // 2

            def step(t, p, turns, x_=True):
                m_prod(t, p)
                m_a(t - 1, 1 - p)
                if x_:
                    m_dst(t + 2, p, turns + 3)
                    m_x(t + 2, p)
                m_index(t - 2, p, turns)

            step(2, 0, 0)
            step(3, 1, 0)
            with v.Fori(2, full + 1) as u:
                step(2 * u, 0, u - 1)
                step(2 * u + 1, 1, u - 1)
            t0 = 2 * (full + 1)
            for t in range(t0, N_TILES):
                step(t, t % 2, (t - 2) // 2, t + 2 < N_TILES)
            m_a(N_TILES - 1, (N_TILES - 1) % 2)
            for t in (N_TILES - 2, N_TILES - 1):
                m_index(t, t % 2, t // 2)

            v.wait_ge(s["weights_w"], 7)
            for g in range(NG):
                add_low(v, g)
            for g in range(NG):
                v.wait_ge(high_in[g], 16)
                after(v, f"low_added{g}", GT)
                for j in range(GT):
                    add_part(v, g, 1, j).then_inc(s["done"], 1)

        @block.tensor
        def _(pe):
            both = lambda h, l, *ix: (h[ix], l[ix])
            full_ = slice(None)
            give(pe, "dn_ps")
            pe.wait_ge(s["const_v"], 5)
            pe.wait_ge(w_in, 16)
            wst = stage[:].rearrange("p k (o h) -> p (k o) h", h=D)
            for t in range(K):
                for k in range(K):
                    ins = pe.transpose(bank[0][:, k * D + t * P:k * D + t * P + P], wst[:, t, k * P:(k + 1) * P], ident[:])
            ins.then_inc(s["wt_ps"], 1)
            pe.wait_ge(y_in, 16)
            for k in range(K):
                for b in range(B):
                    o = (k * B + b) * JP
                    ins = pe.transpose(bank[1][:, o:o + JP], xn[0:JP, b, k * P:(k + 1) * P], ident[0:JP, 0:JP])
            ins.then_inc(s["yT_ps"], 1)
            after(pe, "row_built", 1)
            pe.matmul(bank[6][:, 0:2 * JP + 2], ones_row, row, start=True, stop=True).then_inc(s["row_ps"], 1)
            after(pe, "wt_l", 1)
            after(pe, "yT_l", 1)

            def turn_x(g):
                after(pe, "xn_ready", g + 1)
                after(pe, "eT_l", g)
                for k in range(K):
                    for j in range(GT):
                        ins = pe.transpose(bank[k][:, j * P:(j + 1) * P], xn[:, j, k * P:(k + 1) * P], ident[:])
                    ins.then_inc(s["xt_ps"], 1)

            def project(g):
                after(pe, "xt_l", K * g + K)
                after(pe, "resid", GT * g)
                after(pe, "place_read", g - 1)
                for o in range(K):
                    mm3(pe, bank[2 + o][:], lambda k: both(wt_hi, wt_lo, full_, k, slice(o * P, o * P + P)),
                        lambda k: both(xt_hi, xt_lo, full_, k), K).then_inc(s["xp_ps"], 1)

            def scores(g):
                after(pe, "xp_l", K * g + K)
                b = g // (NG // B)
                for j in range(GT):
                    ins = mm3(pe, bank[0][:, j * JP:(j + 1) * JP],
                              lambda k: both(xp_hi, xp_lo, full_, k, slice(j * P, j * P + P)),
                              lambda k: tuple(w[:, k, bass.ds(b, 1), :].rearrange("p a j -> p (a j)")
                                              for w in (yp_hi, yp_lo)), K)
                ins.then_inc(s["sc_ps"], 1)

            def turn_e(g):
                after(pe, "hT_l", K * (g - 1) + 1)
                after(pe, "sc_exp", g + 1)
                for j in range(GT):
                    ins = pe.transpose(bank[1][0:JP, j * P:(j + 1) * P], s_exp[:, j, :], ident[:])
                ins.then_inc(s["eT_ps"], 1)

            def matched(g):
                after(pe, "eT_l", g + 1)
                after(pe, "rt", RT * (g - 1) + 1)
                b = g // (NG // B)
                for j in range(GT):
                    ins = mm3(pe, bank[2 + j // 2][:, (j % 2) * D:(j % 2) * D + D],
                              lambda k: both(xt_hi, xt_lo, slice(0, JP), 0, slice(j * P, j * P + P)),
                              lambda k: tuple(w[:, bass.ds(b, 1), :].rearrange("p a d -> p (a d)")
                                              for w in (y_hi, y_lo)), 1)
                    if j % 2:
                        ins.then_inc(s["mt_ps"], 1)

            def turn_h(g):
                after(pe, "h_ready", g + 1)
                for k in range(K):
                    for j in range(GT):
                        ins = pe.transpose(bank[1 + 2 * k][:, j * P:(j + 1) * P], hn[:, j, k * P:(k + 1) * P], ident[:])
                    ins.then_inc(s["hT_ps"], 1)

            def router(g):
                after(pe, "hT_l", K * g + K)
                after(pe, "place_read", g)
                mm3(pe, bank[2][0:E, :], lambda k: both(wr_hi, wr_lo, full_, k),
                    lambda k: both(ht_hi, ht_lo, full_, k), K).then_inc(s["lgT_ps"], 1)

            def router_turn(g):
                apart(pe, "lgT_sb", g + 1)
                for j in range(GT):
                    ins = pe.transpose(bank[2][:, j * E:(j + 1) * E], lgT[:, j * P:(j + 1) * P], ident[0:E, 0:E])
                ins.then_inc(s["lg_ps"], 1)

            def rank(g):
                after(pe, "rt", RT * g + RT)
                after(pe, "seen_ready", g)
                if not (isinstance(g, int) and g == NG - 1):
                    after(pe, "resid", GT * g + GT + 2)
                ps = bank[2]
                pe.matmul(ps[:, 0:GT * E], before[:], pick[:].rearrange("p t e -> p (t e)"), start=True, stop=False,
                          skip_group_check=True)
                for j in range(GT - 1):
                    pe.matmul(ps[:, (j + 1) * E:GT * E].rearrange("p (t e) -> p t e", e=E), ones[:],
                              bc_mid(pick[:, j, :], GT - 1 - j), start=False, stop=False, skip_group_check=True)
                pe.matmul(ps[:, 0:GT * E].rearrange("p (t e) -> p t e", e=E), ones[:], bc_mid(seen[:], GT),
                          start=False, stop=True, skip_group_check=True).then_inc(s["rank_ps"], 1)

            def gate_up(g, f):
                n = FC * g + f
                after(pe, "prod", n)
                after(pe, "hT_l", K * g + K)
                for ps, c in ((BG, 0), (BU, 2)):
                    ins = mm3(pe, ps[:], lambda k: both(sw_hi, sw_lo, full_, c + k, slice(f * P, f * P + P)),
                              lambda k: both(ht_hi, ht_lo, full_, k), K)
                ins.then_inc(s["gu_ps"], 1)

            def down(g, f):
                after(pe, "act_l", FC * g + f + 1)
                if f == 0:
                    after(pe, "dn_added", g)
                for j in range(GT):
                    ins = mm3(pe, BD[j // 2][:, (j % 2) * D:(j % 2) * D + D],
                              lambda k: both(act_hi, act_lo, full_, f % 2, slice(j * P, j * P + P)),
                              lambda k: both(sw_hi, sw_lo, full_, 4 + f // 2, slice((f % 2) * D, (f % 2) * D + D)),
                              1, first=f == 0 and j % 2 == 0, last=f == FC - 1, lone=False)
                ins.then_inc(s["dn_ps"], 1)


            def projected_context():
                N = B * JP
                for o in range(K):
                    ins = mm3(pe, bank[7][:, o * N:(o + 1) * N],
                              lambda k: both(wt_hi, wt_lo, full_, k, slice(o * P, o * P + P)),
                              lambda k: both(xp_hi, xp_lo, full_, 0, slice(k * N, k * N + N)), K)
                ins.then_inc(s["yp_ps"], 1)

            def turn(g):
                back, mid, ahead_ = parts_of(g)
                if back:
                    gate_up(g - 1, 0)
                if mid:
                    matched(g)
                if ahead_:
                    turn_x(g + 1)
                if not mid:
                    projected_context()
                if back:
                    gate_up(g - 1, 1)
                    rank(g - 1)
                if ahead_:
                    project(g + 1)
                if not mid:
                    after(pe, "yp_l", 1)
                    after(pe, "row_bc", 2)
                    after(pe, "wr_l", 1)
                if back:
                    gate_up(g - 1, 2)
                    down(g - 1, 0)
                    down(g - 1, 1)
                if ahead_:
                    scores(g + 1)
                if back:
                    gate_up(g - 1, 3)
                if mid:
                    turn_h(g)
                if back:
                    down(g - 1, 2)
                if ahead_:
                    turn_e(g + 1)
                if mid:
                    router(g)
                if back:
                    down(g - 1, 3)
                if mid:
                    router_turn(g)
                if isinstance(g, int) and g == 0:
                    after(pe, "chunk_l", 6)

            turns_of_groups(pe, turn)
            gate_up(NG - 1, 0)
            rank(NG - 1)
            after(pe, "seen_ready", NG)
            pe.matmul(bank[3][:, 0:E], ones[:], seen[:], start=True, stop=True).then_inc(s["cnt_ps"], 1)
            gate_up(NG - 1, 1)
            down(NG - 1, 0)
            gate_up(NG - 1, 2)
            down(NG - 1, 1)
            gate_up(NG - 1, 3)
            down(NG - 1, 2)

            def m_turn_x(t, p, turns):
                pe.wait_ge(tile_in[p], 16 * turns)
                after(pe, "xT_l", t - 1)
                for k in range(K):
                    ins = pe.transpose(bank[2 + p][:, k * P:(k + 1) * P], hr[:, p, k * P:(k + 1) * P], ident[:])
                ins.then_inc(s["xT_ps"], 1)

            def expert_of(t):
                return nc.values_load(t_w[0:1, bass.ds(t, 1)], engines=(mybir.EngineType.PE,), min_val=0,
                                      max_val=E - 1, skip_runtime_bounds_check_because="t_w is held to 0..E-1")

            def weights(e, c, lo_, hi_):
                return tuple(at(w, 3 * e + c)[:, lo_:hi_] for w in (ew_hi, ew_lo))

            def m_up(t, p, e):
                after(pe, "xT_l", t + 1)
                after(pe, "m_prod", t - 1)
                mm3(pe, bank[p][:], lambda k: both(xt_hi, xt_lo, full_, p, slice(k * P, k * P + P)),
                    lambda k: weights(e, k, 0, 512), K).then_inc(s["h1_ps"], 1)

            def m_turn_a(t, p):
                after(pe, "m_prod", t + 1)
                after(pe, "aT_l", t - 1)
                for k in range(K):
                    ins = pe.transpose(bank[4 + p][:, k * P:(k + 1) * P], act[:, p, k * P:(k + 1) * P], ident[:])
                ins.then_inc(s["aT_ps"], 1)

            def m_down(t, p, e):
                after(pe, "aT_l", t + 1)
                after(pe, "y_sb", t - 1)
                mm3(pe, bank[6 + p][:, 0:D], lambda k: both(xp_hi, xp_lo, full_, p, slice(k * P, k * P + P)),
                    lambda k: weights(e, 2, k * D, k * D + D), K).then_inc(s["y2_ps"], 1)

            after(pe, "chunk_l", 6 + WCH)
            m_turn_x(0, 0, 1)
            m_turn_x(1, 1, 1)
            down(NG - 1, FC - 1)
            after(pe, "prod", FC * NG)
            after(pe, "tiles_known", 1)
            m_up(0, 0, expert_of(0))
            m_turn_x(2, 0, 2)
            m_up(1, 1, expert_of(1))
            m_turn_a(0, 0)
            m_turn_x(3, 1, 2)

            def steps(t, n, turns):
                e = {}
                for i in range(n):
                    more = lambda j: not isinstance(t, int) or t + i + j < N_TILES
                    if i < 3:
                        e[i - 2] = expert_of(t + i - 2)
                    m_turn_a(t + i - 1, 1 - i % 2)
                    if more(2):
                        m_turn_x(t + i + 2, i % 2, turns + i // 2)
                    if more(1):
                        e[i + 1] = expert_of(t + i + 1)
                    m_down(t + i - 2, i % 2, e[i - 2])
                    if more(1):
                        m_up(t + i + 1, 1 - i % 2, e[i + 1])

            m_up(2, 0, expert_of(2))
            after(pe, "dn_added", NG)
            steps(2, 2, 3)
            turns_ = (N_TILES - 5) // UNROLL
            with pe.Fori(0, turns_) as u:
                steps(UNROLL * u + 4, UNROLL, UNROLL // 2 * u + 4)
            t0 = UNROLL * turns_ + 4
            steps(t0, N_TILES - t0, t0 // 2 + 2)
            m_turn_a(N_TILES - 1, (N_TILES - 1) % 2)
            for t in (N_TILES - 2, N_TILES - 1):
                m_down(t, t % 2, expert_of(t))


_INS = ["x", "ctx_1024", "mask_BxS2_bk0", "g_xattn", "g_ffn", "L0_xattn_W", "L0_xattn_b", "L0_ffn_w_router",
        "L0_ffn_fc1_w", "L0_ffn_fc2_w", "L0_ffn_gate_w", "L0_ffn_up_w", "L0_ffn_down_w"]


def kernel(**inputs):
    import numpy as _np
    import concourse.bacc as _bacc
    from concourse import mybir as _mybir
    from concourse.bass_utils import run_bass_kernel_spmd as _run

    nc = _bacc.Bacc("TRN2", target_bir_lowering=False, num_devices=1)
    arrays, args = {}, []
    for name in _INS:
        a = _np.ascontiguousarray(inputs[name])
        arrays[f"in_{name}"] = a
        args.append(nc.dram_tensor(f"in_{name}", a.shape, _mybir.dt.from_np(a.dtype), kind="ExternalInput").ap())
    args.append(nc.dram_tensor("out_0", (2, 1024, 256), _mybir.dt.float32, kind="ExternalOutput").ap())
    build(nc, *args)
    r = _run(nc, [arrays], core_ids=[0])
    return r.results[0]["out_0"]
```
